# Optimizing a Trainium2 kernel written in Bass

```python
import numpy as np
import jax
import jax.numpy as jnp

def _softmax(x, axis=-1):
    return jax.nn.softmax(x, axis=axis)

def _gelu(x):
    return jax.nn.gelu(x, approximate=True)

def _silu(x):
    return jax.nn.silu(x)

def _sigmoid(x):
    return jax.nn.sigmoid(x)

def _layernorm(x, axis=-1, eps=1e-05):
    m = jnp.mean(x, axis=axis, keepdims=True)
    v = jnp.var(x, axis=axis, keepdims=True)
    return (x - m) / jnp.sqrt(v + eps)

def _scatter_add(tgt, idx, src, axis=0):
    return tgt.at[idx].add(src)

def _segment_sum(src, seg, n):
    return jax.ops.segment_sum(src, seg, n)
kernel_name = 'mk_adaln_attn_ffn_d1_seqx_r8_a098f4'

def setup_inputs(seed: int=0):
    np.random.seed(seed)
    _w = jnp.asarray

    def _rec_inputs():
        import jax
        import jax.numpy as jnp
        _rk = jax.random.key(seed)
        x = -0.000125 + 0.9999 * jax.random.normal(jax.random.fold_in(_rk, 1), (8, 256, 128), jnp.float32)
        _lenS = 256 - jax.random.randint(jax.random.fold_in(_rk, 7), (8,), 0, max(1, 256 // 4) + 1, jnp.int32)
        _lenS2 = 256 - jax.random.randint(jax.random.fold_in(_rk, 8), (8,), 0, max(1, 256 // 4) + 1, jnp.int32)
        cond_8 = jax.random.uniform(jax.random.fold_in(_rk, 11), (8, 8), jnp.float32, 0.0, 0.983423)
        return (x, cond_8)
    x, cond_8 = _rec_inputs()

    def _L0_cond_setup():
        import jax, jax.numpy as jnp
        import numpy as np
        B, S, D = (16, 256, 128)
        E, H = (8, 256)
        key = jax.random.key(seed)
        ks = jax.random.split(key, 8)
        scale = 0.02
        x = jax.random.normal(ks[0], (B, S, D), dtype=jnp.float32)
        opcode_onehot = jax.random.uniform(ks[1], (B, E), dtype=jnp.float32)
        W_up = jax.random.normal(ks[2], (E, H, D), dtype=jnp.float32) * scale
        b_up = jnp.zeros((E, H), dtype=jnp.float32)
        W_gate = jax.random.normal(ks[3], (E, H, D), dtype=jnp.float32) * scale
        b_gate = jnp.zeros((E, H), dtype=jnp.float32)
        W_down = jax.random.normal(ks[4], (E, D, H), dtype=jnp.float32) * scale
        b_down = jnp.zeros((E, D), dtype=jnp.float32)
        return {'x': x, 'opcode_onehot': opcode_onehot, 'W_up': W_up, 'b_up': b_up, 'W_gate': W_gate, 'b_gate': b_gate, 'W_down': W_down, 'b_down': b_down}
    _L0_cond_all = _L0_cond_setup()
    _L0_cond_in = {k: v for k, v in _L0_cond_all.items() if k in ('W_up', 'b_up', 'W_gate', 'b_gate', 'W_down', 'b_down')}
    del _L0_cond_all

    def _L0_attn_setup():
        import jax, jax.numpy as jnp
        import numpy as np
        NUM_HEADS = 16
        D_MODEL = 128
        HEAD_DIM = D_MODEL // NUM_HEADS
        NEG_INF = -1000000000.0

        def alibi_bidirectional_bias(num_heads, seq_len, dtype=jnp.float32):
            half = num_heads // 2
            base = 24.0 ** (1.0 / half)
            slopes = (1.0 / base ** jnp.arange(1, half + 1, dtype=dtype))[:, None, None]
            pos = jnp.arange(seq_len)
            rel = (pos[None, :] - pos[:, None]).astype(dtype)
            neg = jnp.full((seq_len, seq_len), NEG_INF, dtype=dtype)
            fwd = slopes * jnp.tril(rel) + jnp.triu(neg, 1)
            bwd = slopes * jnp.triu(-rel) + jnp.tril(neg, -1)
            return jnp.concatenate([fwd, bwd], axis=0)
        key = jax.random.key(seed)
        ks = jax.random.split(key, 9)
        B, S, D = (2, 256, D_MODEL)
        sc = 1.0 / np.sqrt(D)
        inp = {'x': jax.random.normal(ks[0], (B, S, D), dtype=jnp.float32)}
        inp['Wq'] = jax.random.normal(ks[1], (D, D), dtype=jnp.float32) * sc
        inp['bq'] = jnp.zeros((D,), dtype=jnp.float32)
        inp['Wk'] = jax.random.normal(ks[2], (D, D), dtype=jnp.float32) * sc
        inp['bk'] = jnp.zeros((D,), dtype=jnp.float32)
        inp['Wv'] = jax.random.normal(ks[3], (D, D), dtype=jnp.float32) * sc
        inp['bv'] = jnp.zeros((D,), dtype=jnp.float32)
        inp['Wf'] = jax.random.normal(ks[4], (D, D), dtype=jnp.float32) * sc
        inp['bf'] = jnp.zeros((D,), dtype=jnp.float32)
        return inp
    _L0_attn_all = _L0_attn_setup()
    _L0_attn_in = {k: v for k, v in _L0_attn_all.items() if k in ('Wq', 'bq', 'Wk', 'bk', 'Wv', 'bv', 'Wf', 'bf')}
    del _L0_attn_all

    def _L0_cond2_setup():
        import jax, jax.numpy as jnp
        import numpy as np
        R = 16
        ALPHA = 32.0
        SCALING = ALPHA / R
        key = jax.random.key(seed)
        ks = jax.random.split(key, 6)
        B, T, C, O, E = (16, 1500, 128, 128, 8)
        x = jax.random.normal(ks[0], (B, T, C), dtype=jnp.float32)
        w = jax.random.uniform(ks[1], (B, E), dtype=jnp.float32)
        W_base = jax.random.normal(ks[2], (O, C), dtype=jnp.float32) * 0.02
        b_base = jax.random.normal(ks[3], (O,), dtype=jnp.float32) * 0.02
        As = jax.random.normal(ks[4], (E, R, C), dtype=jnp.float32) * 0.02
        Bs = jax.random.normal(ks[5], (E, O, R), dtype=jnp.float32) * 0.02
        return {'x': x, 'w': w, 'W_base': W_base, 'b_base': b_base, 'As': As, 'Bs': Bs}
    _L0_cond2_all = _L0_cond2_setup()
    _L0_cond2_in = {k: v for k, v in _L0_cond2_all.items() if k in ('W_base', 'b_base', 'As', 'Bs')}
    del _L0_cond2_all

    def _L0_ffn_setup():
        import jax, jax.numpy as jnp
        import numpy as np
        D_MODEL, D_FF, RANK = (128, 512, 32)
        B, S = (4, 512)
        key = jax.random.key(seed)
        ks = jax.random.split(key, 7)
        return {'x': jax.random.normal(ks[0], (B, S, D_MODEL), dtype=jnp.float32), 'U1': jax.random.normal(ks[1], (D_MODEL, RANK), dtype=jnp.float32) * 0.02, 'V1': jax.random.normal(ks[2], (RANK, D_FF), dtype=jnp.float32) * 0.02, 'b1': jnp.zeros((D_FF,), dtype=jnp.float32), 'U2': jax.random.normal(ks[3], (D_FF, RANK), dtype=jnp.float32) * 0.02, 'V2': jax.random.normal(ks[4], (RANK, D_MODEL), dtype=jnp.float32) * 0.02, 'b2': jnp.zeros((D_MODEL,), dtype=jnp.float32)}
    _L0_ffn_all = _L0_ffn_setup()
    _L0_ffn_in = {k: v for k, v in _L0_ffn_all.items() if k in ('U1', 'V1', 'b1', 'U2', 'V2', 'b2')}
    del _L0_ffn_all
    return {'x': x, 'cond_8': cond_8, 'L0_cond_W_up': _L0_cond_in['W_up'], 'L0_cond_b_up': _L0_cond_in['b_up'], 'L0_cond_W_gate': _L0_cond_in['W_gate'], 'L0_cond_b_gate': _L0_cond_in['b_gate'], 'L0_cond_W_down': _L0_cond_in['W_down'], 'L0_cond_b_down': _L0_cond_in['b_down'], 'L0_attn_Wq': _L0_attn_in['Wq'], 'L0_attn_bq': _L0_attn_in['bq'], 'L0_attn_Wk': _L0_attn_in['Wk'], 'L0_attn_bk': _L0_attn_in['bk'], 'L0_attn_Wv': _L0_attn_in['Wv'], 'L0_attn_bv': _L0_attn_in['bv'], 'L0_attn_Wf': _L0_attn_in['Wf'], 'L0_attn_bf': _L0_attn_in['bf'], 'L0_cond2_W_base': _L0_cond2_in['W_base'], 'L0_cond2_b_base': _L0_cond2_in['b_base'], 'L0_cond2_As': _L0_cond2_in['As'], 'L0_cond2_Bs': _L0_cond2_in['Bs'], 'L0_ffn_U1': _L0_ffn_in['U1'], 'L0_ffn_V1': _L0_ffn_in['V1'], 'L0_ffn_b1': _L0_ffn_in['b1'], 'L0_ffn_U2': _L0_ffn_in['U2'], 'L0_ffn_V2': _L0_ffn_in['V2'], 'L0_ffn_b2': _L0_ffn_in['b2']}

def reference(x, cond_8, L0_cond_W_up, L0_cond_b_up, L0_cond_W_gate, L0_cond_b_gate, L0_cond_W_down, L0_cond_b_down, L0_attn_Wq, L0_attn_bq, L0_attn_Wk, L0_attn_bk, L0_attn_Wv, L0_attn_bv, L0_attn_Wf, L0_attn_bf, L0_cond2_W_base, L0_cond2_b_base, L0_cond2_As, L0_cond2_Bs, L0_ffn_U1, L0_ffn_V1, L0_ffn_b1, L0_ffn_U2, L0_ffn_V2, L0_ffn_b2):
    import jax
    import jax.numpy as jnp

    def _L0_cond_ref(x, opcode_onehot, W_up, b_up, W_gate, b_gate, W_down, b_down):
        import jax, jax.numpy as jnp
        import numpy as np
        B, S, D = (16, 256, 128)
        E, H = (8, 256)
        expert = jnp.argmax(opcode_onehot, axis=-1)
        wu, bu = (W_up[expert], b_up[expert])
        wg, bg = (W_gate[expert], b_gate[expert])
        wd, bd = (W_down[expert], b_down[expert])
        up = jnp.einsum('bsd,bhd->bsh', x, wu) + bu[:, None, :]
        gate = jnp.einsum('bsd,bhd->bsh', x, wg) + bg[:, None, :]
        hidden = jax.nn.silu(up) * gate
        out = jnp.einsum('bsh,bdh->bsd', hidden, wd) + bd[:, None, :]
        return out

    def _L0_attn_ref(x, Wq, bq, Wk, bk, Wv, bv, Wf, bf):
        import jax, jax.numpy as jnp
        import numpy as np
        NUM_HEADS = 16
        D_MODEL = 128
        HEAD_DIM = D_MODEL // NUM_HEADS
        NEG_INF = -1000000000.0

        def alibi_bidirectional_bias(num_heads, seq_len, dtype=jnp.float32):
            half = num_heads // 2
            base = 24.0 ** (1.0 / half)
            slopes = (1.0 / base ** jnp.arange(1, half + 1, dtype=dtype))[:, None, None]
            pos = jnp.arange(seq_len)
            rel = (pos[None, :] - pos[:, None]).astype(dtype)
            neg = jnp.full((seq_len, seq_len), NEG_INF, dtype=dtype)
            fwd = slopes * jnp.tril(rel) + jnp.triu(neg, 1)
            bwd = slopes * jnp.triu(-rel) + jnp.tril(neg, -1)
            return jnp.concatenate([fwd, bwd], axis=0)
        B, S, D = x.shape
        H, hd = (NUM_HEADS, HEAD_DIM)

        def heads(y):
            return y.reshape(B, S, H, hd).transpose(0, 2, 1, 3)
        q = heads(x @ Wq + bq)
        k = heads(x @ Wk + bk)
        v = heads(x @ Wv + bv)
        bias = alibi_bidirectional_bias(H, S, x.dtype)
        scores = jnp.einsum('bhqd,bhkd->bhqk', q, k) * (1.0 / np.sqrt(hd)) + bias[None]
        attn = jax.nn.softmax(scores, axis=-1)
        out = jnp.einsum('bhqk,bhkd->bhqd', attn, v)
        out = out.transpose(0, 2, 1, 3).reshape(B, S, D)
        return out @ Wf + bf

    def _L0_cond2_ref(x, w, W_base, b_base, As, Bs):
        import jax, jax.numpy as jnp
        import numpy as np
        R = 16
        ALPHA = 32.0
        SCALING = ALPHA / R
        out = jnp.einsum('btc,oc->bto', x, W_base) + b_base
        h = jnp.einsum('btc,erc->bter', x, As)
        lora = jnp.einsum('bter,eor,be->bto', h, Bs, w)
        return out + lora * SCALING

    def _L0_ffn_ref(x, U1, V1, b1, U2, V2, b2):
        import jax, jax.numpy as jnp
        import numpy as np
        D_MODEL, D_FF, RANK = (128, 512, 32)
        B, S = (4, 512)
        P = jnp.einsum('bsd,dr->bsr', x, U1)
        H = jax.nn.gelu(jnp.einsum('bsr,rf->bsf', P, V1) + b1)
        Q = jnp.einsum('bsf,fr->bsr', H, U2)
        return jnp.einsum('bsr,rd->bsd', Q, V2) + b2
    x = x + _L0_attn_ref(_L0_cond_ref(x, cond_8, L0_cond_W_up, L0_cond_b_up, L0_cond_W_gate, L0_cond_b_gate, L0_cond_W_down, L0_cond_b_down), L0_attn_Wq, L0_attn_bq, L0_attn_Wk, L0_attn_bk, L0_attn_Wv, L0_attn_bv, L0_attn_Wf, L0_attn_bf)
    x = x + _L0_ffn_ref(_L0_cond2_ref(x, cond_8, L0_cond2_W_base, L0_cond2_b_base, L0_cond2_As, L0_cond2_Bs), L0_ffn_U1, L0_ffn_V1, L0_ffn_b1, L0_ffn_U2, L0_ffn_V2, L0_ffn_b2)
    return x

_drawn_inputs = setup_inputs


def setup_inputs(seed=0):
    import zlib

    import numpy as np

    out = dict(_drawn_inputs(seed))
    spreads = {'L0_cond_b_up': (0.0, 0.8),
     'L0_cond_b_gate': (0.0, 0.8),
     'L0_cond_b_down': (0.0, 0.1),
     'L0_attn_bq': (0.0, 0.8),
     'L0_attn_bk': (0.0, 2.0),
     'L0_attn_bv': (0.0, 0.681),
     'L0_attn_bf': (0.0, 0.8),
     'L0_ffn_b1': (0.0, 2.0),
     'L0_ffn_b2': (0.0, 0.8)}
    factors = {'L0_cond_W_up': 8.0,
     'L0_cond_W_gate': 8.0,
     'L0_cond_W_down': 8.0,
     'L0_attn_Wq': 8.0,
     'L0_attn_Wk': 8.0,
     'L0_cond2_W_base': 8.0,
     'L0_cond2_b_base': 64.0,
     'L0_cond2_As': 8.0,
     'L0_cond2_Bs': 8.0,
     'L0_ffn_U1': 8.0,
     'L0_ffn_V1': 8.0,
     'L0_ffn_U2': 8.0,
     'L0_ffn_V2': 8.0}
    for name, (base, spread) in spreads.items():
        noise = np.random.default_rng([zlib.crc32(name.encode()), seed]).standard_normal(out[name].shape)
        drawn = base * np.exp(spread * noise) if base else spread * noise
        out[name] = jnp.asarray(drawn.astype(out[name].dtype))
    for name, factor in factors.items():
        out[name] = (out[name] * factor).astype(out[name].dtype)
    return out
```

```python
import concourse.bass as bass
from concourse import mybir
from contextlib import ExitStack

B, SEQ, D = 8, 256, 128
HEADS, HD = 16, 8
HALF = HEADS // 2
EXPERTS, RANK_L = 8, 16
FF, RANK = 512, 32
NF = FF // 128
HC = 2
NT = SEQ // 128
SCALE = 1.0 / HD ** 0.5
LORA_SCALE = 32.0 / RANK_L

WU0, WG0, WD0, BU0 = 0, 256, 512, 768
BG0, BD0 = BU0 + HC, BU0 + 2 * HC
WCOLS = BU0 + 2 * HC + 1

A_COLS = {}
_at = 0
for _n, _w in (("wq", 128), ("wk", 128), ("wv", 128), ("wf", 128), ("ident", 128), ("bv", 128),
               ("bq", 1), ("bk", 1), ("bf", 1)):
    A_COLS[_n] = (_at, _at + _w)
    _at += _w
A_TOTAL = _at

F_COLS = {}
_at = 0
for _n, _w in (("base", 128), ("lora_b", 128), ("lora_a", 128), ("u1", 8 * RANK), ("b_base", 1), ("cond", B),
               ("b1", NF), ("u2", NF * RANK), ("v2", 128), ("b2", 1), ("v1", NF * FF)):
    F_COLS[_n] = (_at, _at + _w)
    _at += _w
F_TOTAL = _at

SLOTS = 6
R_STACK = SLOTS * HD
R_MAXROW = 70
R_ALL = R_MAXROW + 2
R_CONST = R_ALL - R_STACK
CH = 12


def adaln_attention_ffn(nc, xT_d, wexp_d, cond_d, pa_d, pf_d, cb_d, qc_d, kc_d, out_d):
    fp32, bf16, u32 = mybir.dt.float32, mybir.dt.bfloat16, mybir.dt.uint32
    ALU, ACT, AX = mybir.AluOpType, mybir.ActivationFunctionType, mybir.AxisListType

    stage_q = nc.dram_tensor("stage_q", [B, SLOTS, 128, SEQ], bf16, kind="Internal").ap()
    stage_k = nc.dram_tensor("stage_k", [B, SLOTS, 128, SEQ], bf16, kind="Internal").ap()
    stage_v = nc.dram_tensor("stage_v", [B, 128, NT * D], fp32, kind="Internal").ap()

    ctx = ExitStack()
    with ctx:
        def sb(name, shape, dt=fp32):
            return ctx.enter_context(nc.sbuf_tensor(name, shape, dt))

        def sem(name):
            return ctx.enter_context(nc.semaphore(name))

        xT = sb("xT", [128, B * SEQ])
        x1 = sb("x1", [128, B * SEQ])
        pa = sb("pa", [128, A_TOTAL])
        pf = sb("pf", [128, F_TOTAL])
        cb = sb("cb", [128, 3 * 128], bf16)
        ident_b, mask_up, mask_lo = cb[:, 0:128], cb[:, 128:256], cb[:, 256:384]
        cond_sb = sb("cond_sb", [B, EXPERTS])
        top = sb("top", [B, 8])
        expert = sb("expert", [B, 8], u32)
        expert_row = sb("expert_row", [1, B], u32)
        wexp = [sb(f"wexp{p}", [128, WCOLS]) for p in range(2)]
        up_half = [sb(f"up_half{p}", [128, 512]) for p in range(2)]
        tanh_up = [sb(f"tanh_up{p}", [128, 512]) for p in range(2)]
        silu_up = [sb(f"silu_up{p}", [128, 512]) for p in range(2)]
        hidden = [sb(f"hidden{p}", [128, 512]) for p in range(2)]
        cT = [sb(f"cT{p}", [128, SEQ]) for p in range(2)]
        qk32 = [sb(f"qk32{p}", [128, 2 * SEQ]) for p in range(2)]
        rest = [sb(f"rest{p}", [128, 2 * SEQ]) for p in range(2)]
        parts = [sb(f"parts{p}", [128, 3, 2, SEQ], bf16) for p in range(2)]
        vrow = [sb(f"vrow{p}", [128, NT * D]) for p in range(2)]
        QS = [sb(f"QS{p}", [R_ALL, HEADS, SEQ], bf16) for p in range(2)]
        KS = [sb(f"KS{p}", [R_ALL, HEADS, SEQ], bf16) for p in range(2)]
        vload = [sb(f"vload{p}", [128, NT * D]) for p in range(2)]
        vaug = [sb(f"vaug{p}", [128, NT, HEADS, 32]) for p in range(2)]
        ones = sb("ones", [128, NT * D])
        mx = [sb(f"mx{p}", [128, HEADS * NT]) for p in range(2)]
        mrow = [sb(f"mrow{h}", [HALF * NT, 2, 128], bf16) for h in range(2)]
        PB = [[sb(f"PB{g}{c}", [128, 512]) for c in range(3)] for g in range(2)]
        OS = [sb(f"OS{h}", [128, 512]) for h in range(2)]
        rden = [sb(f"rden{h}", [128, NT * HALF]) for h in range(2)]
        On = sb("On", [128, NT, D])
        OnT = sb("OnT", [128, SEQ])
        lora_m = sb("lora_m", [128, RANK])
        lora_w = sb("lora_w", [128, B * RANK])
        G = sb("G", [128, B * RANK])
        pbias = sb("pbias", [128, 1])
        P4 = sb("P4", [128, 512])
        H = [sb(f"H{f}", [128, 512]) for f in range(NF)]
        Q4 = [sb(f"Q4{j}", [128, 512]) for j in range(2)]
        Y = [sb(f"Y{j}", [128, 512]) for j in range(2)]

        bank = [ctx.enter_context(nc.psum_tensor(f"bank{n}", [128, 512], fp32)) for n in range(8)]
        up_ps, gate_ps = bank[0:2], bank[2:4]
        c_ps, qk_ps, v_ps = bank[4], bank[5], bank[6]
        S_ps, T_ps, O_ps, M_ps = bank[0:2], bank[2:4], bank[4:6], bank[6:8]

        def A(name):
            return pa[:, A_COLS[name][0]:A_COLS[name][1]]

        def F(name):
            return pf[:, F_COLS[name][0]:F_COLS[name][1]]

        v1z = F("v1").rearrange("p (j n) -> p j n", j=NF)
        u2 = F("u2").rearrange("p (f r) -> p f r", f=NF)

        cond_in, pa_in, pf_in, cb_in, const_in, row_in = map(
            sem, ("cond_in", "pa_in", "pf_in", "cb_in", "const_in", "row_in"))
        w_in = [sem(f"w_in{p}") for p in range(2)]
        staged = [sem(f"staged{p}") for p in range(2)]
        qk_in = [[sem(f"qk_in{h}{p}") for p in range(2)] for h in range(2)]
        v_in = [sem(f"v_in{p}") for p in range(2)]
        mrow_in = [sem(f"mrow_in{h}") for h in range(2)]
        top_done, expert_done = sem("top_done"), sem("expert_done")
        up_done, gate_done, half_done, tanh_done, silu_done, hid_done, down_done, c_taken = map(
            sem, ("up_done", "gate_done", "half_done", "tanh_done", "silu_done", "hid_done", "down_done", "c_taken"))
        qkmm_done, vmm_done, qk32_done, v_taken, hi_done, rest_done, mid_done, low_done = map(
            sem, ("qkmm_done", "vmm_done", "qk32_done", "v_taken", "hi_done", "rest_done", "mid_done", "low_done"))
        zero_done = sem("zero_done")
        lm_done, lm_taken, lw_done, g_done, g_taken, pb_done = map(
            sem, ("lm_done", "lm_taken", "lw_done", "g_done", "g_taken", "pb_done"))
        s_done, max_done, t_done, exp_done, pv_done, va_done = map(
            sem, ("s_done", "max_done", "t_done", "exp_done", "pv_done", "va_done"))
        o_taken = [sem(f"o_taken{h}") for h in range(2)]
        mt_done = [sem(f"mt_done{h}") for h in range(2)]
        mt_hi = [sem(f"mt_hi{h}") for h in range(2)]
        mt_taken = [sem(f"mt_taken{h}") for h in range(2)]
        dt_done = [sem(f"dt_done{h}") for h in range(2)]
        rden_done = [sem(f"rden_done{h}") for h in range(2)]
        dt_taken = [sem(f"dt_taken{h}") for h in range(2)]
        ont_done, ont_taken, wf_done, x1_done = map(sem, ("ont_done", "ont_taken", "wf_done", "x1_done"))
        p_done, p_taken, h_done, gelu_done, q_done, q_taken, y_done, y_taken = map(
            sem, ("p_done", "p_taken", "h_done", "gelu_done", "q_done", "q_taken", "y_done", "y_taken"))
        out_done = [sem(f"out_done{p}") for p in range(2)]

        block = ctx.enter_context(nc.Block())

        def wait(eng, s, value):
            if isinstance(value, int) and value <= 0:
                return
            eng.wait_ge(s, value)

        def chunk_kind(side, half, c):
            full = (c > 0) if side == "S" else (c < 2)
            if side == "S":
                part = (1 if full else 0) if half == 0 else (0 if full else 1)
                mask = mask_up if half == 0 else mask_lo
                pair = c - 1
            else:
                part = (0 if full else 1) if half == 0 else (1 if full else 0)
                mask = mask_lo if half == 0 else mask_up
                pair = c
            return part, full, pair, mask

        @block.sync
        def _(sp):
            sp.dma_start(cond_sb[:, :], cond_d).then_inc(cond_in, 16)
            sp.dma_start(pa[:, :], pa_d).then_inc(pa_in, 16)
            sp.wait_ge(expert_done, 1)
            sp.dma_start(expert_row[0:1, :], expert[:, 0:1]).then_inc(row_in, 16)
            sp.wait_ge(row_in, 16)

            def load_expert(b, p, half_b):
                wait(sp, c_taken, b - 1)
                e = sp.value_load(expert_row[0:1, bass.ds(b, 1)], min_val=0, max_val=EXPERTS - 1)
                sp.dma_start(wexp[p][:, :], wexp_d[bass.ds(e, 1), :, :].rearrange("a p n -> (a p) n"))\
                    .then_inc(w_in[p], 16)
                sp.dma_start(xT[:, bass.ds(b * SEQ, SEQ)], xT_d[:, bass.ds(b * SEQ, SEQ)]).then_inc(w_in[p], 16)

            def store_stage(b, p):
                wait(sp, low_done, b + 1)
                sq = stage_q[bass.ds(b, 1)].rearrange("a j p s -> p (a j) s")
                sk = stage_k[bass.ds(b, 1)].rearrange("a j p s -> p (a j) s")
                sp.dma_start(sq[:, 0:3, :], parts[p][:, 0:3, 0, :]).then_inc(staged[p], 16)
                sp.dma_start(sq[:, 3:5, :], parts[p][:, 0:2, 0, :]).then_inc(staged[p], 16)
                sp.dma_start(sq[:, 5:6, :], parts[p][:, 0:1, 0, :]).then_inc(staged[p], 16)
                sp.dma_start(sk[:, 0:3, :], parts[p][:, 0:1, 1, :].broadcast_to([128, 3, SEQ])).then_inc(staged[p], 16)
                sp.dma_start(sk[:, 3:5, :], parts[p][:, 1:2, 1, :].broadcast_to([128, 2, SEQ])).then_inc(staged[p], 16)
                sp.dma_start(sk[:, 5:6, :], parts[p][:, 2:3, 1, :]).then_inc(staged[p], 16)
                wait(sp, v_taken, b + 1)
                sp.dma_start(stage_v[bass.ds(b, 1)].rearrange("a p n -> (a p) n"), vrow[p][:, :])\
                    .then_inc(staged[p], 16)

            for k in range(4):
                load_expert(k, k % 2, k // 2)
                if k == 1:
                    sp.dma_start(cb[:, :], cb_d).then_inc(cb_in, 16)
                    for p in range(2):
                        sp.dma_start(QS[p][R_STACK:R_ALL, :, :], qc_d).then_inc(const_in, 16)
                        sp.dma_start(KS[p][R_STACK:R_ALL, :, :], kc_d).then_inc(const_in, 16)
                    sp.dma_start(pf[:, :], pf_d).then_inc(pf_in, 16)
                if k >= 3:
                    store_stage(k - 3, (k - 3) % 2)
            with sp.Fori(0, 2) as t:
                for p in range(2):
                    load_expert(2 * t + 4 + p, p, t + 2)
                    store_stage(2 * t + 1 + p, 1 - p)
            for b in range(5, B):
                store_stage(b, b % 2)

            def load_half(b, p, h):
                rows = slice(h * HALF, (h + 1) * HALF)
                for src, dst in ((stage_q, QS), (stage_k, KS)):
                    view = src[bass.ds(b, 1)].rearrange("a j (d h) s -> (a j d) h s", d=HD)
                    sp.dma_start(dst[p][0:R_STACK, rows, :], view[:, rows, :]).then_inc(qk_in[h][p], 16)

            def load_v(b, p):
                sp.dma_start(vload[p][:, :], stage_v[bass.ds(b, 1)].rearrange("a p n -> (a p) n"))\
                    .then_inc(v_in[p], 16)

            def max_rows(b, p, h):
                wait(sp, mt_taken[h], b + 1)
                for r in range(2):
                    sp.dma_start(QS[p][R_MAXROW + r:R_MAXROW + r + 1, h * HALF:(h + 1) * HALF, :],
                                 mrow[h][:, r, :]).then_inc(mrow_in[h], 16)

            for p in range(2):
                sp.wait_ge(staged[p], 7 * 16 * B // 2)
            for b in range(2):
                load_half(b, b, 0)
                load_half(b, b, 1)
                load_v(b, b)

            def attention_loads(i, p, last):
                max_rows(i, p, 1)
                if not last:
                    wait(sp, t_done, CH * i + 6)
                    load_half(i + 2, p, 0)
                    wait(sp, va_done, i + 1)
                    load_v(i + 2, p)

            max_rows(0, 0, 0)
            attention_loads(0, 0, False)
            max_rows(1, 1, 0)
            wait(sp, t_done, CH)
            load_half(2, 0, 1)
            with sp.Fori(0, 2) as t:
                for p in (1, 0):
                    i = 2 * t + (1 if p else 2)
                    attention_loads(i, p, False)
                    max_rows(i + 1, 1 - p, 0)
                    wait(sp, t_done, CH * i + CH)
                    load_half(i + 2, p, 1)
            attention_loads(5, 1, False)
            max_rows(6, 0, 0)
            wait(sp, t_done, CH * 6)
            load_half(7, 1, 1)
            attention_loads(6, 0, True)
            max_rows(7, 1, 0)
            attention_loads(7, 1, True)

            view = out_d.rearrange("p (q j s) -> p q j s", q=2, j=4)
            for j in range(4):
                wait(sp, y_taken, j + 1)
                sp.dma_start(view[:, :, j, :], Y[j % 2][:, :].rearrange("p (q s) -> p q s", q=2))\
                    .then_inc(out_done[j % 2], 16)
            for p in range(2):
                sp.wait_ge(out_done[p], 32)

        @block.gpsimd
        def _(pool):
            for p in range(2):
                pool.memset(vaug[p][:, :, :, HD:32], 0.0).then_inc(zero_done, 1)
            pool.memset(ones[:, :], 1.0).then_inc(zero_done, 1)
            pool.wait_ge(zero_done, 3)
            for p in range(2):
                pool.memset(vaug[p][:, :, :, HD:HD + 1], 1.0).then_inc(zero_done, 1)

            def remainder(b, p):
                wait(pool, hi_done, b + 1)
                wait(pool, low_done, b - 1)
                pool.tensor_tensor(rest[p][:, :].rearrange("p (a s) -> p a s", a=2),
                                   qk32[p][:, :].rearrange("p (a s) -> p a s", a=2),
                                   parts[p][:, 0, :, :], ALU.subtract).then_inc(rest_done, 1)

            for b in range(2):
                remainder(b, b)
            with pool.Fori(0, 2) as t:
                for p in range(2):
                    remainder(2 * t + 2 + p, p)
            for b in range(6, B):
                remainder(b, b % 2)

            def spread_v(b, p, count):
                pool.wait_ge(v_in[p], 16 * count)
                wait(pool, pv_done, 4 * b - 4)
                pool.tensor_tensor(vaug[p][:, :, :, 0:HD].rearrange("p t h d -> p (t h) d"),
                                   vload[p][:, :].rearrange("p (n d) -> p n d", d=HD),
                                   ones[:, :].rearrange("p (n d) -> p n d", d=HD), ALU.mult).then_inc(va_done, 1)

            for b in range(2):
                spread_v(b, b, 1)
            with pool.Fori(0, 3) as t:
                for p in range(2):
                    spread_v(2 * t + 2 + p, p, t + 2)

        @block.scalar
        def _(act):
            def tanh_of(b, p):
                wait(act, half_done, 2 * b + 2)
                nc.scalar.activation(tanh_up[p][:, :], up_half[p][:, :], ACT.Tanh).then_inc(tanh_done, 1)

            def take_c(b, p):
                wait(act, down_done, b + 1)
                nc.scalar.activation(cT[p][:, :], c_ps[:, 0:SEQ], ACT.Identity, bias=wexp[p][:, BD0:BD0 + 1])\
                    .then_inc(c_taken, 1)

            def high_part(b, p, count):
                wait(act, qk32_done, 2 * b + 2)
                wait(act, staged[p], count)
                nc.scalar.activation(parts[p][:, 0, :, :], qk32[p][:, :].rearrange("p (a s) -> p a s", a=2),
                                     ACT.Copy).then_inc(hi_done, 1)

            def mid_part(b, p):
                wait(act, rest_done, b + 1)
                nc.scalar.activation(parts[p][:, 1, :, :], rest[p][:, :].rearrange("p (a s) -> p a s", a=2),
                                     ACT.Copy).then_inc(mid_done, 1)

            for k in range(10):
                if k == 4:
                    with act.Fori(0, 2) as t:
                        for p in range(2):
                            b = 2 * t + 4 + p
                            tanh_of(b, p)
                            take_c(b - 1, 1 - p)
                            high_part(b - 2, p, 112 * (t + 1))
                            mid_part(b - 2, p)
                if 4 <= k < B:
                    continue
                if k < B:
                    tanh_of(k, k % 2)
                if 1 <= k <= B:
                    take_c(k - 1, (k - 1) % 2)
                if k >= 2:
                    b = k - 2
                    high_part(b, b % 2, 112 * (b // 2))
                    mid_part(b, b % 2)

            act.wait_ge(lm_done, 1)
            nc.scalar.activation(lora_m[:, :], M_ps[0][:, 0:RANK], ACT.Copy, scale=LORA_SCALE).then_inc(lm_taken, 1)
            act.wait_ge(g_done, 2)
            nc.scalar.activation(G[:, :], M_ps[1][:, 0:B * RANK], ACT.Copy).then_inc(g_taken, 1)
            nc.scalar.activation(pbias[:, :], M_ps[0][:, 64:65], ACT.Copy).then_inc(pb_done, 1)

            def exp_chunk(i, g, c):
                wait(act, t_done, CH * i + 3 * g + c + 1)
                if c == 0:
                    wait(act, pv_done, 4 * i + g - 1)
                nc.scalar.activation(PB[g % 2][c][:, :], T_ps[(3 * g + c) % 2][:, :], ACT.Exp).then_inc(exp_done, 1)

            def take_o(i, h):
                wait(act, pv_done, 4 * i + 2 * h + 2)
                wait(act, dt_done[h], i)
                nc.scalar.activation(OS[h][:, :], O_ps[h][:, :], ACT.Copy).then_inc(o_taken[h], 1)

            def take_ont(i):
                wait(act, ont_done, i + 1)
                wait(act, wf_done, i)
                nc.scalar.activation(OnT[:, :], M_ps[0][:, 0:SEQ], ACT.Copy).then_inc(ont_taken, 1)

            def step(i, finish):
                for g in range(4):
                    for c in range(3):
                        exp_chunk(i, g, c)
                        if finish and (g, c) == (1, 0):
                            take_o(i - 1, 1)
                        if (g, c) == (3, 0):
                            take_o(i, 0)
                        if finish and (g, c) == (3, 1):
                            take_ont(i - 1)

            step(0, False)
            with act.Fori(0, 3) as t:
                step(2 * t + 1, True)
                step(2 * t + 2, True)
            step(7, True)
            take_o(7, 1)
            take_ont(7)

            for j in range(4):
                for f in range(NF):
                    act.wait_ge(h_done, NF * j + f + 1)
                    if j >= 1:
                        act.wait_ge(q_done, j)
                    nc.scalar.activation(H[f][:, :], bank[f][:, :], ACT.Gelu_apprx_tanh,
                                         bias=F("b1")[:, f:f + 1]).then_inc(gelu_done, 1)

        @block.vector
        def _(dve):
            dve.wait_ge(cond_in, 16)
            nc.vector.max(top[:, :], cond_sb[:, :]).then_inc(top_done, 1)
            dve.wait_ge(top_done, 1)
            nc.vector.max_index(expert[:, :], top[:, :], cond_sb[:, :]).then_inc(expert_done, 1)

            def half_up(b, p):
                wait(dve, up_done, b + 1)
                for h in range(HC):
                    nc.vector.tensor_scalar(up_half[p][:, h * SEQ:(h + 1) * SEQ], up_ps[p][:, h * SEQ:(h + 1) * SEQ],
                                            wexp[p][:, BU0 + h:BU0 + h + 1], 0.5, ALU.add, ALU.mult)\
                        .then_inc(half_done, 1)

            def hide(b, p):
                wait(dve, tanh_done, b + 1)
                nc.vector.scalar_tensor_tensor(out=silu_up[p][:, :], in0=tanh_up[p][:, :], scalar=1.0,
                                               in1=up_half[p][:, :], op0=ALU.add, op1=ALU.mult).then_inc(silu_done, 1)
                wait(dve, silu_done, b + 1)
                wait(dve, gate_done, b + 1)
                for h in range(HC):
                    cols = slice(h * SEQ, (h + 1) * SEQ)
                    last = nc.vector.scalar_tensor_tensor(out=hidden[p][:, cols], in0=gate_ps[p][:, cols],
                                                          scalar=wexp[p][:, BG0 + h:BG0 + h + 1],
                                                          in1=silu_up[p][:, cols], op0=ALU.add, op1=ALU.mult)
                last.then_inc(hid_done, 1)

            def take_qkv(b, p, count):
                wait(dve, qkmm_done, b + 1)
                nc.vector.tensor_scalar(qk32[p][:, 0:SEQ], qk_ps[:, 0:SEQ], A("bq"), SCALE, ALU.add, ALU.mult)\
                    .then_inc(qk32_done, 1)
                nc.vector.tensor_scalar(qk32[p][:, SEQ:2 * SEQ], qk_ps[:, SEQ:2 * SEQ], A("bk"), None, ALU.add)\
                    .then_inc(qk32_done, 1)
                wait(dve, vmm_done, b + 1)
                wait(dve, staged[p], count)
                nc.vector.tensor_tensor(vrow[p][:, :].rearrange("p (t n) -> p t n", t=NT),
                                        v_ps[:, 0:NT * D].rearrange("p (t n) -> p t n", t=NT),
                                        A("bv").rearrange("p (a n) -> p a n", a=1).broadcast_to([128, NT, D]),
                                        ALU.add).then_inc(v_taken, 1)

            def low_part(b, p):
                wait(dve, mid_done, b + 1)
                nc.vector.tensor_tensor(parts[p][:, 2, :, :], rest[p][:, :].rearrange("p (a s) -> p a s", a=2),
                                        parts[p][:, 1, :, :], ALU.subtract).then_inc(low_done, 1)

            dve.wait_ge(pa_in, 16)
            for k in range(11):
                if k == 4:
                    with dve.Fori(0, 2) as t:
                        for p in range(2):
                            b = 2 * t + 4 + p
                            hide(b - 1, 1 - p)
                            half_up(b, p)
                            take_qkv(b - 2, p, 112 * (t + 1))
                            low_part(b - 3, 1 - p)
                if 4 <= k < B:
                    continue
                if 1 <= k <= B:
                    hide(k - 1, (k - 1) % 2)
                if k < B:
                    half_up(k, k % 2)
                if 2 <= k < B + 2:
                    b = k - 2
                    take_qkv(b, b % 2, 112 * (b // 2))
                if k >= 3:
                    low_part(k - 3, (k - 3) % 2)

            dve.wait_ge(lm_taken, 1)
            nc.vector.tensor_tensor(lora_w[:, :].rearrange("p (b r) -> p b r", b=B),
                                    lora_m[:, :].rearrange("p (a r) -> p a r", a=1).broadcast_to([128, B, RANK]),
                                    F("cond").rearrange("p (b a) -> p b a", a=1).broadcast_to([128, B, RANK]),
                                    ALU.mult).then_inc(lw_done, 1)

            def reduce_chunk(i, p, g, c):
                n = 3 * g + c
                part, full, pair, _ = chunk_kind("S", g // 2, c)
                wait(dve, s_done, CH * i + n + 1)
                cols = mx[p][:, :].rearrange("p (h t) -> p h t", t=NT)
                if full:
                    head = 4 * g + 2 * pair
                    out = cols[:, head:head + 2, part]
                    src = S_ps[n % 2][:, :].rearrange("p (h s) -> p h s", h=2)
                else:
                    out = cols[:, 4 * g:4 * g + 4, part]
                    src = S_ps[n % 2][:, :].rearrange("p (h s) -> p h s", h=4)
                if n in (0, 6):
                    wait(dve, mt_done[n // 6], i - 1)
                nc.vector.tensor_reduce(out, src, AX.X, ALU.max).then_inc(max_done, 1)

            def split_max(i, h):
                wait(dve, mt_done[h], i + 1)
                wait(dve, mrow_in[h], 32 * i)
                nc.vector.tensor_scalar(mrow[h][:, 0, :], M_ps[1][0:HALF * NT, 0:128], -1.0, None, ALU.mult)\
                    .then_inc(mt_hi[h], 1)
                wait(dve, mt_hi[h], i + 1)
                nc.vector.scalar_tensor_tensor(out=mrow[h][:, 1, :], in0=M_ps[1][0:HALF * NT, 0:128], scalar=-1.0,
                                               in1=mrow[h][:, 0, :], op0=ALU.mult, op1=ALU.subtract)\
                    .then_inc(mt_taken[h], 1)

            def normalise(i, h):
                wait(dve, dt_done[h], i + 1)
                src = M_ps[h][:, :].rearrange("p (t h r) -> p t h r", t=NT, r=32)
                rd = rden[h][:, :].rearrange("p (t h) -> p t h", t=NT)
                nc.vector.reciprocal(rd, src[:, :, :, HD]).then_inc(rden_done[h], 1)
                wait(dve, rden_done[h], i + 1)
                wait(dve, ont_done, i)
                nc.vector.tensor_tensor(
                    On[:, :, h * 64:(h + 1) * 64].rearrange("p t (h d) -> p t h d", d=HD), src[:, :, :, 0:HD],
                    rden[h][:, :].rearrange("p (t h a) -> p t h a", t=NT, a=1).broadcast_to([128, NT, HALF, HD]),
                    ALU.mult).then_inc(dt_taken[h], 1)

            def residual(i):
                wait(dve, wf_done, i + 1)
                nc.vector.scalar_tensor_tensor(out=x1[:, bass.ds(i * SEQ, SEQ)], in0=M_ps[0][:, 0:SEQ],
                                               scalar=A("bf"), in1=xT[:, bass.ds(i * SEQ, SEQ)],
                                               op0=ALU.add, op1=ALU.add).then_inc(x1_done, 1)

            def step(i, p, ahead, now, finish):
                for g in range(4):
                    for c in range(3):
                        if ahead:
                            reduce_chunk(i + 1, 1 - p, g, c)
                        if now and (g, c) == (0, 0):
                            split_max(i, 1)
                        if ahead and (g, c) == (2, 1):
                            split_max(i + 1, 0)
                    if finish and g == 1:
                        normalise(i - 1, 0)
                        normalise(i - 1, 1)
                if finish:
                    residual(i - 1)

            step(-1, 1, True, False, False)
            step(0, 0, True, True, False)
            with dve.Fori(0, 3) as t:
                step(2 * t + 1, 1, True, True, True)
                step(2 * t + 2, 0, True, True, True)
            step(7, 1, False, True, True)
            step(8, 0, False, False, True)

            dve.wait_ge(p_done, 1)
            nc.vector.tensor_scalar(P4[:, :], M_ps[0][:, :], pbias[:, 0:1], None, ALU.add).then_inc(p_taken, 1)
            for j in range(4):
                dve.wait_ge(q_done, j + 1)
                if j >= 2:
                    dve.wait_ge(y_done, j - 1)
                nc.vector.tensor_copy(Q4[j % 2][:, :], O_ps[j % 2][:, :]).then_inc(q_taken, 1)
                dve.wait_ge(y_done, j + 1)
                if j >= 2:
                    dve.wait_ge(out_done[j % 2], 16)
                nc.vector.scalar_tensor_tensor(
                    out=Y[j % 2][:, :].rearrange("p (q s) -> p q s", q=2),
                    in0=M_ps[j % 2][:, :].rearrange("p (q s) -> p q s", q=2), scalar=F("b2"),
                    in1=x1[:, :].rearrange("p (q j s) -> p q j s", q=2, j=4)[:, :, j, :],
                    op0=ALU.add, op1=ALU.add).then_inc(y_taken, 1)

        @block.tensor
        def _(pe):
            def up_gate(b, p, count):
                pe.wait_ge(w_in[p], 32 * count)
                for base, ps, done, free, per in ((WU0, up_ps, up_done, half_done, 2), (WG0, gate_ps, gate_done, hid_done, 1)):
                    wait(pe, free, per * (b - 1))
                    for h in range(HC):
                        last = nc.tensor.matmul(ps[p][:, h * SEQ:(h + 1) * SEQ],
                                                wexp[p][:, base + h * 128:base + (h + 1) * 128],
                                                xT[:, bass.ds(b * SEQ, SEQ)], start=True, stop=True)
                    last.then_inc(done, 1)

            def down(b, p):
                wait(pe, hid_done, b + 1)
                wait(pe, c_taken, b)
                for h in range(HC):
                    last = nc.tensor.matmul(c_ps[:, 0:SEQ], wexp[p][:, WD0 + h * 128:WD0 + (h + 1) * 128],
                                            hidden[p][:, h * SEQ:(h + 1) * SEQ], start=(h == 0), stop=(h == HC - 1))
                last.then_inc(down_done, 1)

            def project(b, p):
                wait(pe, c_taken, b + 1)
                wait(pe, qk32_done, 2 * b)
                nc.tensor.matmul(qk_ps[:, 0:SEQ], A("wq"), cT[p][:, :], start=True, stop=True)
                nc.tensor.matmul(qk_ps[:, SEQ:2 * SEQ], A("wk"), cT[p][:, :], start=True, stop=True)\
                    .then_inc(qkmm_done, 1)
                wait(pe, v_taken, b)
                for t in range(NT):
                    last = nc.tensor.matmul(v_ps[:, t * D:(t + 1) * D], cT[p][:, t * 128:(t + 1) * 128], A("wv"),
                                            start=True, stop=True)
                last.then_inc(vmm_done, 1)

            pe.wait_ge(pa_in, 16)
            for k in range(10):
                if k == 4:
                    with pe.Fori(0, 2) as t:
                        for p in range(2):
                            b = 2 * t + 4 + p
                            up_gate(b, p, t + 3)
                            down(b - 1, 1 - p)
                            project(b - 2, p)
                if 4 <= k < B:
                    continue
                if k < B:
                    up_gate(k, k % 2, k // 2 + 1)
                if 1 <= k <= B:
                    down(k - 1, (k - 1) % 2)
                if k >= 2:
                    project(k - 2, (k - 2) % 2)

            pe.wait_ge(pf_in, 16)
            pe.wait_ge(v_taken, B)
            nc.tensor.matmul(M_ps[0][:, 0:RANK], F("lora_b"), F("u1")[:, 0:RANK], start=True, stop=True)\
                .then_inc(lm_done, 1)
            pe.wait_ge(lw_done, 1)
            nc.tensor.matmul(M_ps[1][:, 0:B * RANK], F("lora_a"), lora_w[:, :], start=True, stop=False)
            nc.tensor.matmul(M_ps[1][:, 0:B * RANK], F("base"), F("u1"), start=False, stop=True).then_inc(g_done, 1)
            nc.tensor.matmul(M_ps[0][:, 64:65], F("u1")[:, 0:128], F("b_base"), start=True, stop=True)\
                .then_inc(g_done, 1)
            pe.wait_ge(g_taken, 1)
            pe.wait_ge(pb_done, 1)
            pe.wait_ge(hid_done, B)
            pe.wait_ge(qk32_done, 2 * B)
            pe.wait_ge(cb_in, 16)
            pe.wait_ge(const_in, 64)

            def scores(side, ps, stationary, moving, rows, g, c):
                part, full, pair, mask = chunk_kind(side, g // 2, c)
                nh = 2 if full else 4
                view = ps[:, :].rearrange("p (h s) -> p h s", h=nh)
                diag = view[:, :, part * 128:(part + 1) * 128] if full else view
                nc.tensor.matmul(diag, ident_b, mask.rearrange("p (a s) -> p a s", a=1).broadcast_to([128, nh, 128]),
                                 start=True, stop=False, skip_group_check=True)
                for n in range(nh):
                    head = 4 * g + (2 * pair if full else 0) + n
                    rhs = moving[0:rows, head, :] if full else moving[0:rows, head, part * 128:(part + 1) * 128]
                    last = nc.tensor.matmul(view[:, n, :], stationary[0:rows, head, part * 128:(part + 1) * 128], rhs,
                                            start=False, stop=(n == nh - 1), skip_group_check=True)
                return last

            def s_chunk(i, p, g, c, count):
                n = 3 * g + c
                if n in (0, 6):
                    pe.wait_ge(qk_in[n // 6][p], 32 * count)
                wait(pe, max_done, CH * i + n - 1)
                scores("S", S_ps[n % 2], QS[p], KS[p], R_MAXROW, g, c).then_inc(s_done, 1)

            def t_chunk(i, p, g, c):
                n = 3 * g + c
                if n in (0, 6):
                    wait(pe, mrow_in[n // 6], 32 * (i + 1))
                wait(pe, exp_done, CH * i + n - 1)
                scores("T", T_ps[n % 2], KS[p], QS[p], R_ALL, g, c).then_inc(t_done, 1)

            def pv(i, p, g):
                h = g // 2
                if g == 0:
                    wait(pe, va_done, i + 1)
                if g % 2 == 0:
                    wait(pe, o_taken[h], i)
                wait(pe, exp_done, CH * i + 3 * g + 3)
                cols = (g % 2) * SEQ
                for c, part in ((0, h), (2, 1 - h)):
                    for j in range(4):
                        v = vaug[p][:, part, 4 * g + j, :]
                        if c == 0:
                            last = nc.tensor.matmul(O_ps[h][32 * j:32 * j + 32, cols:cols + SEQ], v,
                                                    PB[g % 2][j // 2][:, (j % 2) * SEQ:(j % 2 + 1) * SEQ],
                                                    start=(g % 2 == 0), stop=False, skip_group_check=True)
                        else:
                            at = cols + part * 128
                            last = nc.tensor.matmul(O_ps[h][32 * j:32 * j + 32, at:at + 128], v,
                                                    PB[g % 2][2][:, j * 128:(j + 1) * 128],
                                                    start=False, stop=True, skip_group_check=True)
                last.then_inc(pv_done, 1)

            def turn_max(i, p, h):
                wait(pe, max_done, CH * i + 6 * (h + 1))
                if h == 1:
                    wait(pe, mt_taken[0], i + 1)
                else:
                    wait(pe, dt_taken[1], i - 1)
                nc.tensor.transpose(M_ps[1][0:HALF * NT, 0:128], mx[p][:, h * HALF * NT:(h + 1) * HALF * NT], A("ident"))\
                    .then_inc(mt_done[h], 1)

            def turn_o(i, h):
                wait(pe, o_taken[h], i + 1)
                if h == 0:
                    wait(pe, x1_done, i)
                else:
                    wait(pe, mt_taken[1], min(i + 2, B) if isinstance(i, int) else i + 2)
                for t in range(NT):
                    for g in range(2):
                        at = g * SEQ + t * 128
                        last = nc.tensor.transpose(M_ps[h][:, t * 256 + g * 128:t * 256 + (g + 1) * 128],
                                                   OS[h][:, at:at + 128], A("ident"))
                last.then_inc(dt_done[h], 1)

            def turn_on(i):
                for h in range(2):
                    wait(pe, dt_taken[h], i + 1)
                for t in range(NT):
                    last = nc.tensor.transpose(M_ps[0][:, t * 128:(t + 1) * 128], On[:, t, :], A("ident"))
                last.then_inc(ont_done, 1)

            def out_project(i):
                wait(pe, ont_taken, i + 1)
                nc.tensor.matmul(M_ps[0][:, 0:SEQ], A("wf"), OnT[:, :], start=True, stop=True).then_inc(wf_done, 1)

            def step(i, p, count, ahead, now, finish):
                for g in range(4):
                    for c in range(3):
                        if ahead:
                            s_chunk(i + 1, 1 - p, g, c, count)
                        if now:
                            t_chunk(i, p, g, c)
                        if now and (g, c) == (0, 0):
                            turn_max(i, p, 1)
                        if ahead and (g, c) == (2, 1):
                            turn_max(i + 1, 1 - p, 0)
                    if finish and g == 0:
                        pv(i - 1, 1 - p, 3)
                    if now and g >= 1:
                        pv(i, p, g - 1)
                    if finish and g == 1:
                        turn_o(i - 1, 0)
                        turn_o(i - 1, 1)
                    if finish and g == 2:
                        turn_on(i - 1)
                if finish:
                    out_project(i - 1)

            step(-1, 1, 1, True, False, False)
            step(0, 0, 1, True, True, False)
            with pe.Fori(0, 3) as t:
                step(2 * t + 1, 1, t + 2, True, True, True)
                step(2 * t + 2, 0, t + 2, True, True, True)
            step(7, 1, 0, False, True, True)
            step(8, 0, 0, False, False, True)

            pe.wait_ge(x1_done, B)
            for q in range(2):
                for j in range(4):
                    b = 4 * q + j
                    last = nc.tensor.matmul(M_ps[0][32 * j:32 * j + 32, q * SEQ:(q + 1) * SEQ],
                                            G[:, b * RANK:(b + 1) * RANK], x1[:, b * SEQ:(b + 1) * SEQ],
                                            start=(q == 0), stop=True, skip_group_check=True)
            last.then_inc(p_done, 1)
            pe.wait_ge(p_taken, 1)

            def ff_up(j):
                for f in range(NF):
                    if j >= 1:
                        pe.wait_ge(gelu_done, NF * (j - 1) + f + 1)
                    nc.tensor.matmul(bank[f][:, :], v1z[:, j, f * 128:(f + 1) * 128], P4[:, :],
                                     start=True, stop=True).then_inc(h_done, 1)

            ff_up(0)
            for j in range(4):
                if j < 3:
                    ff_up(j + 1)
                if j >= 2:
                    pe.wait_ge(q_taken, j - 1)
                pe.wait_ge(gelu_done, NF * (j + 1))
                for f in range(NF):
                    last = nc.tensor.matmul(O_ps[j % 2][32 * f:32 * f + 32, :], u2[:, f, :], H[f][:, :],
                                            start=True, stop=True)
                last.then_inc(q_done, 1)
                pe.wait_ge(q_taken, j + 1)
                if j >= 2:
                    pe.wait_ge(y_taken, j - 1)
                nc.tensor.matmul(M_ps[j % 2][:, :], F("v2"), Q4[j % 2][:, :], start=True, stop=True)\
                    .then_inc(y_done, 1)


def _packed(inputs):
    import numpy as np

    f32 = np.float32
    g = {k: np.asarray(v) for k, v in inputs.items()}
    xT = np.ascontiguousarray(g["x"].reshape(B * SEQ, D).T)

    def hidden_bias(v):
        return v.reshape(EXPERTS, HC, 128).transpose(0, 2, 1)

    wexp = np.concatenate([
        g["L0_cond_W_up"].transpose(0, 2, 1), g["L0_cond_W_gate"].transpose(0, 2, 1),
        g["L0_cond_W_down"].reshape(EXPERTS, D, HC, 128).transpose(0, 3, 2, 1).reshape(EXPERTS, 128, HC * D),
        hidden_bias(g["L0_cond_b_up"]), hidden_bias(g["L0_cond_b_gate"]), g["L0_cond_b_down"][:, :, None]], axis=2)

    def by_d(w):
        return w.reshape(w.shape[:-1] + (HEADS, HD)).swapaxes(-1, -2).reshape(w.shape)

    pa = np.concatenate([
        by_d(g["L0_attn_Wq"]), by_d(g["L0_attn_Wk"]), g["L0_attn_Wv"], g["L0_attn_Wf"], np.eye(128, dtype=f32),
        np.tile(g["L0_attn_bv"][None], (128, 1)), by_d(g["L0_attn_bq"])[:, None], by_d(g["L0_attn_bk"])[:, None],
        g["L0_attn_bf"][:, None]], axis=1)

    v1 = np.zeros((NF, RANK, NF, FF), f32)
    for j in range(NF):
        v1[j, :, j] = g["L0_ffn_V1"]
    pf = np.concatenate([
        g["L0_cond2_W_base"], g["L0_cond2_Bs"].transpose(1, 0, 2).reshape(D, EXPERTS * RANK_L),
        g["L0_cond2_As"].reshape(EXPERTS * RANK_L, D), np.tile(g["L0_ffn_U1"], (1, B)),
        g["L0_cond2_b_base"][:, None], np.repeat(g["cond_8"].T, RANK_L, axis=0), g["L0_ffn_b1"].reshape(NF, 128).T,
        g["L0_ffn_U2"].reshape(NF, 128, RANK).transpose(1, 0, 2).reshape(128, NF * RANK),
        np.tile(g["L0_ffn_V2"], (NF, 1)), g["L0_ffn_b2"][:, None], v1.reshape(128, NF * FF)], axis=1)

    bf = np.dtype("bfloat16")
    neg = f32(-1e9)
    tri = np.arange(128)
    cb = np.concatenate([np.eye(128, dtype=f32), np.where(tri[None] > tri[:, None], neg, f32(0)),
                         np.where(tri[None] < tri[:, None], neg, f32(0))], axis=1).astype(bf)

    base = 24.0 ** (1.0 / HALF)
    slope = (f32(1.0) / f32(base) ** np.arange(1, HALF + 1, dtype=f32)).astype(f32)
    signed = np.concatenate([slope, -slope])
    three = []
    left = signed.copy()
    for _ in range(3):
        three.append(left.astype(bf).astype(f32))
        left = left - three[-1]
    pos = np.arange(SEQ, dtype=f32)
    qc = np.zeros((R_CONST, HEADS, SEQ), f32)
    kc = np.zeros((R_CONST, HEADS, SEQ), f32)
    for n, s in enumerate(three):
        qc[n], kc[n] = s[:, None], pos[None]
        qc[3 + n], kc[3 + n] = -pos[None], s[:, None]
    kc[R_MAXROW - R_STACK:] = 1.0
    return [xT, wexp, g["cond_8"], pa, pf, cb, qc.astype(bf), kc.astype(bf)]


_INS = ["xT", "wexp", "cond", "pa", "pf", "cb", "qc", "kc"]


def kernel(**inputs):
    import numpy as _np
    import concourse.bacc as _bacc
    from concourse import mybir as _mybir
    from concourse.bass_utils import run_bass_kernel_spmd as _run

    nc = _bacc.Bacc("TRN2", target_bir_lowering=False, num_devices=1)
    arrays, args = {}, []
    for name, a in zip(_INS, _packed(inputs)):
        a = _np.ascontiguousarray(a)
        arrays[f"in_{name}_dram"] = a
        args.append(nc.dram_tensor(f"in_{name}_dram", a.shape, _mybir.dt.from_np(a.dtype), kind="ExternalInput").ap())
    args.append(nc.dram_tensor("out_0_dram", (D, B * SEQ), _mybir.dt.float32, kind="ExternalOutput").ap())
    adaln_attention_ffn(nc, *args)
    r = _run(nc, [arrays], core_ids=[0])
    got = r.results[0]["out_0_dram"]
    return _np.ascontiguousarray(_np.asarray(got).T).reshape(B, SEQ, D)
```

```python
import concourse.bass as bass
from concourse import mybir
from contextlib import ExitStack

B, SEQ, D = 8, 256, 128
HEADS, HD = 16, 8
HALF = HEADS // 2
EXPERTS, RANK_L = 8, 16
FF, RANK = 512, 32
NF = FF // 128
HC = 2
NT = SEQ // 128
SCALE = 1.0 / HD ** 0.5
LORA_SCALE = 32.0 / RANK_L

BU0, BG0, BD0, WU0 = 0, HC, 2 * HC, 2 * HC + 1
WG0, WD0, WCOLS = WU0 + HC * 128, WU0 + 2 * HC * 128, WU0 + 3 * HC * 128

A_COLS = {}
_at = 0
for _n, _w in (("wq", 128), ("wk", 128), ("wv", 128), ("wf", 128), ("ident", 128), ("bv", 128),
               ("bq", 1), ("bk", 1), ("bf", 1)):
    A_COLS[_n] = (_at, _at + _w)
    _at += _w
A_TOTAL = _at

F_COLS = {}
_at = 0
for _n, _w in (("base", 128), ("lora_b", 128), ("lora_a", 128), ("u1", 8 * RANK), ("b_base", 1), ("cond", B),
               ("b1", NF), ("u2", NF * RANK), ("v2", 128), ("b2", 1), ("v1", FF)):
    F_COLS[_n] = (_at, _at + _w)
    _at += _w
F_TOTAL = _at

SLOTS = 6
STAGES = 4
R_STACK = SLOTS * HD
R_MAXROW = 70
R_ALL = R_MAXROW + 2
R_CONST = R_ALL - R_STACK
CH = 12
S0_AT = 4


def adaln_attention_ffn(nc, xT_d, wexp_d, cond_d, pa_d, pf_d, cb_d, qc_d, kc_d, out_d):
    fp32, bf16, u32 = mybir.dt.float32, mybir.dt.bfloat16, mybir.dt.uint32
    ALU, ACT, AX = mybir.AluOpType, mybir.ActivationFunctionType, mybir.AxisListType

    stage_q = nc.dram_tensor("stage_q", [B, SLOTS, 128, SEQ], bf16, kind="Internal").ap()
    stage_k = nc.dram_tensor("stage_k", [B, SLOTS, 128, SEQ], bf16, kind="Internal").ap()
    stage_v = nc.dram_tensor("stage_v", [B, 128, NT * D], fp32, kind="Internal").ap()

    ctx = ExitStack()
    with ctx:
        def sb(name, shape, dt=fp32):
            return ctx.enter_context(nc.sbuf_tensor(name, shape, dt))

        def sem(name):
            return ctx.enter_context(nc.semaphore(name))

        xT = sb("xT", [128, B * SEQ])
        x1 = sb("x1", [128, B * SEQ])
        pa = sb("pa", [128, A_TOTAL])
        pf = sb("pf", [128, F_TOTAL])
        cb = sb("cb", [128, 3 * 128], bf16)
        ident_b, mask_up, mask_lo = cb[:, 0:128], cb[:, 128:256], cb[:, 256:384]
        cond_sb = sb("cond_sb", [B, EXPERTS])
        top = sb("top", [B, 8])
        expert = sb("expert", [B, 8], u32)
        wexp = [sb(f"wexp{b}", [128, WCOLS]) for b in range(B)]
        bq_scaled = sb("bq_scaled", [128, 1])
        up_half = [sb(f"up_half{p}", [128, 512]) for p in range(2)]
        tanh_up = [sb(f"tanh_up{p}", [128, 512]) for p in range(2)]
        silu_up = [sb(f"silu_up{p}", [128, 512]) for p in range(2)]
        hidden = [sb(f"hidden{p}", [128, 512]) for p in range(2)]
        cT = [sb(f"cT{p}", [128, SEQ]) for p in range(2)]
        qk32 = [sb(f"qk32{p}", [128, 2 * SEQ]) for p in range(2)]
        rest = [sb(f"rest{p}", [128, 2 * SEQ]) for p in range(2)]
        parts = [sb(f"parts{p}", [128, 3, 2, SEQ], bf16) for p in range(STAGES)]
        vrow = [sb(f"vrow{p}", [128, NT * D]) for p in range(STAGES)]
        QS = [sb(f"QS{p}", [R_ALL, HEADS, SEQ], bf16) for p in range(2)]
        KS = [sb(f"KS{p}", [R_ALL, HEADS, SEQ], bf16) for p in range(2)]
        vload = [sb(f"vload{p}", [128, NT * D]) for p in range(2)]
        vaug = [sb(f"vaug{p}", [128, NT, HEADS, 32]) for p in range(2)]
        mx = [sb(f"mx{p}", [128, HEADS * NT]) for p in range(2)]
        mrow = [sb(f"mrow{h}", [HALF * NT, 2, 128], bf16) for h in range(2)]
        PB = [[sb(f"PB{g}{c}", [128, 512]) for c in range(3)] for g in range(4)]
        OS = [sb(f"OS{h}", [128, 512]) for h in range(2)]
        rden = [sb(f"rden{h}", [128, NT * HALF]) for h in range(2)]
        On = sb("On", [128, NT, D])
        OnT = sb("OnT", [128, SEQ])
        lora_m = sb("lora_m", [128, RANK])
        lora_w = sb("lora_w", [128, B * RANK])
        G = sb("G", [128, B * RANK])
        pbias = sb("pbias", [128, 1])
        P32 = sb("P32", [128, 512])
        Prest = sb("Prest", [128, 512])
        Pparts = sb("Pparts", [128, 3, 512], bf16)
        Pstack = [sb(f"Pstack{j}", [128, 512], bf16) for j in range(4)]
        v1_parts = sb("v1_parts", [128, 3, FF], bf16)
        v1_rest = sb("v1_rest", [128, FF])
        v1_first = sb("v1_first", [128, FF], bf16)
        v1_second = sb("v1_second", [128, FF], bf16)
        H = [[wexp[NF * p + f][:, 0:512] for f in range(NF)] for p in range(2)]
        Q4 = [sb(f"Q4{j}", [128, 512]) for j in range(2)]
        Y = [sb(f"Y{j}", [128, 512]) for j in range(2)]

        bank = [ctx.enter_context(nc.psum_tensor(f"bank{n}", [128, 512], fp32)) for n in range(8)]
        up_ps = bank[2:4]
        gate_ps, c_ps, qk_ps, v_ps = bank[4:8]
        S_ps, T_ps, O_ps, M_ps = bank[0:2], bank[2:4], bank[4:6], bank[6:8]

        turned_max = M_ps[1][0:HALF * NT, 0:128]

        def A(name):
            return pa[:, A_COLS[name][0]:A_COLS[name][1]]

        def F(name):
            return pf[:, F_COLS[name][0]:F_COLS[name][1]]

        u2 = F("u2").rearrange("p (f r) -> p f r", f=NF)

        cond_in, pa_in, pf_in, cb_in, const_in = map(sem, ("cond_in", "pa_in", "pf_in", "cb_in", "const_in"))
        x_in = [sem(f"x_in{n}") for n in range(3)]
        w_in = [sem(f"w_in{b}") for b in range(B)]
        w_rest_in = sem("w_rest_in")
        staged = [sem(f"staged{p}") for p in range(STAGES)]
        qk_in = [[sem(f"qk_in{h}{p}") for p in range(2)] for h in range(2)]
        v_in = [sem(f"v_in{p}") for p in range(2)]
        mrow_in = [sem(f"mrow_in{h}") for h in range(2)]
        top_done, expert_done = sem("top_done"), sem("expert_done")
        up_done, gate_done, half_done, tanh_done, silu_done, hid_done, down_done, c_taken = map(
            sem, ("up_done", "gate_done", "half_done", "tanh_done", "silu_done", "hid_done", "down_done", "c_taken"))
        qkmm_done, vmm_done, qk32_done, v_taken, hi_done, rest_done, mid_done, low_done = map(
            sem, ("qkmm_done", "vmm_done", "qk32_done", "v_taken", "hi_done", "rest_done", "mid_done", "low_done"))
        zero_done, bq_done, v1_done, v1_stacked = map(sem, ("zero_done", "bq_done", "v1_done", "v1_stacked"))
        lm_done, lm_taken, lw_done, g_done, g_taken, pb_done = map(
            sem, ("lm_done", "lm_taken", "lw_done", "g_done", "g_taken", "pb_done"))
        s_done, max_done, t_done, exp_done, pv_done, va_done = map(
            sem, ("s_done", "max_done", "t_done", "exp_done", "pv_done", "va_done"))
        o_taken = [sem(f"o_taken{h}") for h in range(2)]
        mt_done = [sem(f"mt_done{h}") for h in range(2)]
        mt_hi = [sem(f"mt_hi{h}") for h in range(2)]
        mt_taken = [sem(f"mt_taken{h}") for h in range(2)]
        dt_done = [sem(f"dt_done{h}") for h in range(2)]
        rden_done = [sem(f"rden_done{h}") for h in range(2)]
        dt_taken = [sem(f"dt_taken{h}") for h in range(2)]
        ont_done, ont_taken, wf_done, x1_done = map(sem, ("ont_done", "ont_taken", "wf_done", "x1_done"))
        p_done, p32_done, pchain, stack_done, h_done, gelu_done, q_done, q_taken, y_done, y_taken = map(
            sem, ("p_done", "p32_done", "pchain", "stack_done", "h_done", "gelu_done", "q_done", "q_taken", "y_done", "y_taken"))
        out_done = [sem(f"out_done{p}") for p in range(2)]

        block = ctx.enter_context(nc.Block())

        def wait(eng, s, value):
            if isinstance(value, int) and value <= 0:
                return
            eng.wait_ge(s, value)

        def chunk_kind(side, half, c):
            full = (c > 0) if side == "S" else (c < 2)
            if side == "S":
                part = (1 if full else 0) if half == 0 else (0 if full else 1)
                mask = mask_up if half == 0 else mask_lo
                pair = c - 1
            else:
                part = (0 if full else 1) if half == 0 else (1 if full else 0)
                mask = mask_lo if half == 0 else mask_up
                pair = c
            return part, full, pair, mask

        @block.sync
        def _(sp):
            sp.dma_start(cond_sb[:, :], cond_d).then_inc(cond_in, 16)
            sp.wait_ge(expert_done, 1)
            for b in range(B):
                e = sp.value_load(expert[b:b + 1, 0:1], min_val=0, max_val=EXPERTS - 1)
                for c0, c1 in ((0, WG0), (WG0, WCOLS)) if b == 0 else ((0, WCOLS),):
                    sp.dma_start(wexp[b][:, c0:c1], wexp_d[bass.ds(e, 1), :, c0:c1].rearrange("a p n -> (a p) n"))\
                        .then_inc(w_in[b] if c0 == 0 else w_rest_in, 16)
                if b == 3:
                    sp.dma_start(pf[:, :], pf_d).then_inc(pf_in, 16)
            sp.dma_start(cb[:, :], cb_d).then_inc(cb_in, 16)
            for p in range(2):
                sp.dma_start(QS[p][R_STACK:R_ALL, :, :], qc_d).then_inc(const_in, 16)
                sp.dma_start(KS[p][R_STACK:R_ALL, :, :], kc_d).then_inc(const_in, 16)

            def store_stage(b):
                sp.wait_ge(low_done, b + 1)
                sq = stage_q[b].rearrange("j p s -> p j s")
                sk = stage_k[b].rearrange("j p s -> p j s")
                sp.dma_start(sq[:, 0:3, :], parts[b % STAGES][:, 0:3, 0, :]).then_inc(staged[b % STAGES], 16)
                sp.dma_start(sq[:, 3:5, :], parts[b % STAGES][:, 0:2, 0, :]).then_inc(staged[b % STAGES], 16)
                sp.dma_start(sq[:, 5:6, :], parts[b % STAGES][:, 0:1, 0, :]).then_inc(staged[b % STAGES], 16)
                sp.dma_start(sk[:, 0:3, :], parts[b % STAGES][:, 0:1, 1, :].broadcast_to([128, 3, SEQ])).then_inc(staged[b % STAGES], 16)
                sp.dma_start(sk[:, 3:5, :], parts[b % STAGES][:, 1:2, 1, :].broadcast_to([128, 2, SEQ])).then_inc(staged[b % STAGES], 16)
                sp.dma_start(sk[:, 5:6, :], parts[b % STAGES][:, 2:3, 1, :]).then_inc(staged[b % STAGES], 16)
                sp.wait_ge(v_taken, b + 1)
                sp.dma_start(stage_v[b], vrow[b % STAGES][:, :]).then_inc(staged[b % STAGES], 16)

            def load_half(b, p, h):
                rows = slice(h * HALF, (h + 1) * HALF)
                for src, dst in ((stage_q, QS), (stage_k, KS)):
                    view = src[bass.ds(b, 1)].rearrange("a j (d h) s -> (a j d) h s", d=HD)
                    sp.dma_start(dst[p][0:R_STACK, rows, :], view[:, rows, :]).then_inc(qk_in[h][p], 16)

            def load_v(b, p):
                sp.dma_start(vload[p][:, :], stage_v[bass.ds(b, 1)].rearrange("a p n -> (a p) n"))\
                    .then_inc(v_in[p], 16)

            def max_rows(b, p, h):
                wait(sp, mt_taken[h], b + 1)
                for r in range(2):
                    sp.dma_start(QS[p][R_MAXROW + r:R_MAXROW + r + 1, h * HALF:(h + 1) * HALF, :],
                                 mrow[h][:, r, :]).then_inc(mrow_in[h], 16)

            for b in range(B - 1):
                store_stage(b)
                if b < 2:
                    sp.wait_ge(staged[b], 7 * 16)
                    load_half(b, b, 0)
                    load_half(b, b, 1)
                    load_v(b, b)
                if b == S0_AT:
                    max_rows(0, 0, 0)

            def attention_loads(i, p, last):
                max_rows(i, p, 1)
                if isinstance(i, int) and i == 0:
                    store_stage(B - 1)
                    for s in range(STAGES):
                        sp.wait_ge(staged[s], 7 * 16 * B // STAGES)
                if not last:
                    wait(sp, t_done, CH * i + 6)
                    load_half(i + 2, p, 0)
                    wait(sp, va_done, i + 1)
                    load_v(i + 2, p)

            attention_loads(0, 0, False)
            max_rows(1, 1, 0)
            wait(sp, t_done, CH)
            load_half(2, 0, 1)
            with sp.Fori(0, 2) as t:
                for p in (1, 0):
                    i = 2 * t + (1 if p else 2)
                    attention_loads(i, p, False)
                    max_rows(i + 1, 1 - p, 0)
                    wait(sp, t_done, CH * i + CH)
                    load_half(i + 2, p, 1)
            attention_loads(5, 1, False)
            max_rows(6, 0, 0)
            wait(sp, t_done, CH * 6)
            load_half(7, 1, 1)
            attention_loads(6, 0, True)
            max_rows(7, 1, 0)
            attention_loads(7, 1, True)

            view = out_d.rearrange("p (q j s) -> p q j s", q=2, j=4)
            for j in range(4):
                wait(sp, y_taken, j + 1)
                sp.dma_start(view[:, :, j, :], Y[j % 2][:, :].rearrange("p (q s) -> p q s", q=2))\
                    .then_inc(out_done[j % 2], 16)
            for p in range(2):
                sp.wait_ge(out_done[p], 32)

        @block.gpsimd
        def _(pool):
            for p in range(2):
                pool.memset(vaug[p][:, :, :, HD:32], 0.0).then_inc(zero_done, 1)
            pool.memset(v1_second[:, :], 0.0).then_inc(zero_done, 1)
            pool.wait_ge(zero_done, 3)
            for p in range(2):
                pool.memset(vaug[p][:, :, :, HD:HD + 1], 1.0).then_inc(zero_done, 1)

            def remainder(b, p):
                pool.wait_ge(hi_done, b + 1)
                wait(pool, low_done, b - 1)
                pool.tensor_tensor(rest[p][:, :].rearrange("p (a s) -> p a s", a=2),
                                   qk32[p][:, :].rearrange("p (a s) -> p a s", a=2),
                                   parts[b % STAGES][:, 0, :, :], ALU.subtract).then_inc(rest_done, 1)

            def spread_v(b, p):
                pool.wait_ge(v_in[p], 16 * (b // 2 + 1))
                wait(pool, pv_done, 4 * b - 4)
                pool.tensor_copy(vaug[p][:, :, :, 0:HD],
                                 vload[p][:, :].rearrange("p (t h d) -> p t h d", t=NT, d=HD)).then_inc(va_done, 1)

            def split_v1():
                pool.wait_ge(pf_in, 16)
                pool.tensor_copy(v1_parts[:, 0, :], F("v1")).then_inc(v1_done, 1)
                pool.wait_ge(v1_done, 1)
                pool.tensor_tensor(v1_rest[:, :], F("v1"), v1_parts[:, 0, :], ALU.subtract).then_inc(v1_done, 1)
                pool.wait_ge(v1_done, 2)
                pool.tensor_copy(v1_parts[:, 1, :], v1_rest[:, :]).then_inc(v1_done, 1)
                pool.wait_ge(v1_done, 3)
                pool.tensor_tensor(v1_parts[:, 2, :], v1_rest[:, :], v1_parts[:, 1, :], ALU.subtract)\
                    .then_inc(v1_done, 1)

            for b in range(B):
                remainder(b, b % 2)
            spread_v(0, 0)
            spread_v(1, 1)
            split_v1()

            for b in range(2, B):
                spread_v(b, b % 2)

        @block.scalar
        def _(act):
            act.dma_start(xT[:, 0:SEQ], xT_d[:, 0:SEQ]).then_inc(x_in[0], 16)
            act.wait_ge(expert_done, 1)
            act.dma_start(pa[:, :], pa_d).then_inc(pa_in, 16)
            act.dma_start(xT[:, SEQ:4 * SEQ], xT_d[:, SEQ:4 * SEQ]).then_inc(x_in[1], 16)
            act.dma_start(xT[:, 4 * SEQ:], xT_d[:, 4 * SEQ:]).then_inc(x_in[2], 16)

            def tanh_of(b, p):
                act.wait_ge(half_done, 2 * b + 2)
                nc.scalar.activation(tanh_up[p][:, :], up_half[p][:, :], ACT.Tanh).then_inc(tanh_done, 1)

            def take_c(b, p):
                act.wait_ge(down_done, b + 1)
                nc.scalar.activation(cT[p][:, :], c_ps[:, 0:SEQ], ACT.Identity, bias=wexp[b][:, BD0:BD0 + 1])\
                    .then_inc(c_taken, 1)

            def take_qk(b, p):
                act.wait_ge(qkmm_done, b + 1)
                wait(act, rest_done, b - 1)
                nc.scalar.activation(qk32[p][:, 0:SEQ], qk_ps[:, 0:SEQ], ACT.Identity, bias=bq_scaled[:, 0:1],
                                     scale=SCALE).then_inc(qk32_done, 1)
                nc.scalar.activation(qk32[p][:, SEQ:2 * SEQ], qk_ps[:, SEQ:2 * SEQ], ACT.Identity, bias=A("bk"))\
                    .then_inc(qk32_done, 1)

            def high_part(b, p):
                act.wait_ge(qk32_done, 2 * b + 2)
                wait(act, staged[b % STAGES], 7 * 16 * (b // STAGES))
                nc.scalar.activation(parts[b % STAGES][:, 0, :, :], qk32[p][:, :].rearrange("p (a s) -> p a s", a=2),
                                     ACT.Copy).then_inc(hi_done, 1)

            def mid_part(b, p):
                act.wait_ge(rest_done, b + 1)
                nc.scalar.activation(parts[b % STAGES][:, 1, :, :], rest[p][:, :].rearrange("p (a s) -> p a s", a=2),
                                     ACT.Copy).then_inc(mid_done, 1)

            def fold_lora():
                act.wait_ge(lm_done, 1)
                nc.scalar.activation(lora_m[:, :], S_ps[0][:, 0:RANK], ACT.Copy, scale=LORA_SCALE)\
                    .then_inc(lm_taken, 1)

            def fold_base():
                act.wait_ge(g_done, 2)
                nc.scalar.activation(G[:, :], S_ps[1][:, 0:B * RANK], ACT.Copy).then_inc(g_taken, 1)
                nc.scalar.activation(pbias[:, :], S_ps[0][:, 64:65], ACT.Copy).then_inc(pb_done, 1)

            for k in range(B + 1):
                if k < B:
                    tanh_of(k, k % 2)
                if 1 <= k <= B:
                    take_c(k - 1, (k - 1) % 2)
                if k >= 2:
                    mid_part(k - 2, k % 2)
                if k == 1:
                    act.wait_ge(bq_done, 1)
                if 1 <= k <= B:
                    take_qk(k - 1, (k - 1) % 2)
                    high_part(k - 1, (k - 1) % 2)
                if k == 2:
                    fold_lora()
                if k == 3:
                    fold_base()

            def exp_chunk(i, g, c):
                wait(act, t_done, CH * i + 3 * g + c + 1)
                if c == 0:
                    wait(act, pv_done, 4 * i + g - 3)
                nc.scalar.activation(PB[g][c][:, :], T_ps[(3 * g + c) % 2][:, :], ACT.Exp).then_inc(exp_done, 1)

            def take_o(i, h):
                wait(act, pv_done, 4 * i + 2 * h + 2)
                nc.scalar.activation(OS[h][:, :], O_ps[h][:, :], ACT.Copy).then_inc(o_taken[h], 1)

            def take_ont(i):
                wait(act, ont_done, i + 1)
                nc.scalar.activation(OnT[:, :], M_ps[0][:, 0:SEQ], ACT.Copy).then_inc(ont_taken, 1)

            def step(i, finish):
                for g in range(4):
                    for c in range(3):
                        exp_chunk(i, g, c)
                        if isinstance(i, int) and i == 0 and (g, c) == (0, 0):
                            mid_part(B - 1, (B - 1) % 2)
                        if finish and (g, c) == (1, 0):
                            take_o(i - 1, 1)
                        if (g, c) == (3, 0):
                            take_o(i, 0)
                        if finish and (g, c) == (3, 1):
                            take_ont(i - 1)

            step(0, False)
            with act.Fori(0, 3) as t:
                step(2 * t + 1, True)
                step(2 * t + 2, True)
            step(7, True)
            take_o(7, 1)

            for j in range(4):
                for f in range(NF):
                    if (j, f) == (1, 3):
                        take_ont(7)
                    n = NF * j + f
                    act.wait_ge(h_done, n + 1)
                    if j >= 2:
                        act.wait_ge(q_done, j - 1)
                    nc.scalar.activation(H[j % 2][f], bank[1 + n % 3][:, :], ACT.Gelu_apprx_tanh,
                                         bias=F("b1")[:, f:f + 1]).then_inc(gelu_done, 1)

        @block.vector
        def _(dve):
            dve.wait_ge(cond_in, 16)
            nc.vector.max(top[:, :], cond_sb[:, :]).then_inc(top_done, 1)
            dve.wait_ge(top_done, 1)
            nc.vector.max_index(expert[:, :], top[:, :], cond_sb[:, :]).then_inc(expert_done, 1)

            def half_up(b, p):
                dve.wait_ge(up_done, b + 1)
                for h in range(HC):
                    nc.vector.tensor_scalar(up_half[p][:, h * SEQ:(h + 1) * SEQ], up_ps[p][:, h * SEQ:(h + 1) * SEQ],
                                            wexp[b][:, BU0 + h:BU0 + h + 1], 0.5, ALU.add, ALU.mult)\
                        .then_inc(half_done, 1)

            def hide(b, p):
                dve.wait_ge(tanh_done, b + 1)
                nc.vector.scalar_tensor_tensor(out=silu_up[p][:, :], in0=tanh_up[p][:, :], scalar=1.0,
                                               in1=up_half[p][:, :], op0=ALU.add, op1=ALU.mult).then_inc(silu_done, 1)
                dve.wait_ge(silu_done, b + 1)
                dve.wait_ge(gate_done, b + 1)
                for h in range(HC):
                    cols = slice(h * SEQ, (h + 1) * SEQ)
                    last = nc.vector.scalar_tensor_tensor(out=hidden[p][:, cols], in0=gate_ps[:, cols],
                                                          scalar=wexp[b][:, BG0 + h:BG0 + h + 1],
                                                          in1=silu_up[p][:, cols], op0=ALU.add, op1=ALU.mult)
                last.then_inc(hid_done, 1)

            def take_v(b, p):
                dve.wait_ge(vmm_done, b + 1)
                wait(dve, staged[b % STAGES], 7 * 16 * (b // STAGES))
                nc.vector.tensor_tensor(vrow[b % STAGES][:, :].rearrange("p (t n) -> p t n", t=NT),
                                        v_ps[:, 0:NT * D].rearrange("p (t n) -> p t n", t=NT),
                                        A("bv").rearrange("p (a n) -> p a n", a=1).broadcast_to([128, NT, D]),
                                        ALU.add).then_inc(v_taken, 1)

            def low_part(b, p):
                dve.wait_ge(mid_done, b + 1)
                nc.vector.tensor_tensor(parts[b % STAGES][:, 2, :, :], rest[p][:, :].rearrange("p (a s) -> p a s", a=2),
                                        parts[b % STAGES][:, 1, :, :], ALU.subtract).then_inc(low_done, 1)

            def stack_v1():
                dve.wait_ge(v1_done, 4)
                dve.wait_ge(zero_done, 3)
                nc.vector.tensor_copy(v1_first[0:96, :], v1_parts[0:96, 0, :])
                nc.vector.tensor_copy(v1_first[96:128, :], v1_parts[96:128, 1, :])
                nc.vector.tensor_copy(v1_second[0:32, :], v1_parts[0:32, 2, :])
                nc.vector.tensor_copy(v1_second[32:64, :], v1_parts[32:64, 1, :]).then_inc(v1_stacked, 1)

            def weigh_lora():
                dve.wait_ge(lm_taken, 1)
                nc.vector.tensor_tensor(lora_w[:, :].rearrange("p (b r) -> p b r", b=B),
                                        lora_m[:, :].rearrange("p (a r) -> p a r", a=1).broadcast_to([128, B, RANK]),
                                        F("cond").rearrange("p (b a) -> p b a", a=1).broadcast_to([128, B, RANK]),
                                        ALU.mult).then_inc(lw_done, 1)

            def reduce_chunk(i, p, g, c):
                n = 3 * g + c
                part, full, pair, _ = chunk_kind("S", g // 2, c)
                wait(dve, s_done, CH * i + n + 1)
                cols = mx[p][:, :].rearrange("p (h t) -> p h t", t=NT)
                if full:
                    head = 4 * g + 2 * pair
                    out = cols[:, head:head + 2, part]
                    src = S_ps[n % 2][:, :].rearrange("p (h s) -> p h s", h=2)
                else:
                    out = cols[:, 4 * g:4 * g + 4, part]
                    src = S_ps[n % 2][:, :].rearrange("p (h s) -> p h s", h=4)
                if n in (0, 6):
                    wait(dve, mt_done[n // 6], i - 1)
                nc.vector.tensor_reduce(out, src, AX.X, ALU.max).then_inc(max_done, 1)

            def split_max(i, h):
                wait(dve, mt_done[h], i + 1)
                wait(dve, mrow_in[h], 32 * i)
                nc.vector.tensor_scalar(mrow[h][:, 0, :], turned_max, -1.0, None, ALU.mult)\
                    .then_inc(mt_hi[h], 1)
                wait(dve, mt_hi[h], i + 1)
                nc.vector.scalar_tensor_tensor(out=mrow[h][:, 1, :], in0=turned_max, scalar=-1.0,
                                               in1=mrow[h][:, 0, :], op0=ALU.mult, op1=ALU.subtract)\
                    .then_inc(mt_taken[h], 1)

            def normalise(i, h):
                wait(dve, dt_done[h], i + 1)
                src = M_ps[h][:, :].rearrange("p (t h r) -> p t h r", t=NT, r=32)
                rd = rden[h][:, :].rearrange("p (t h) -> p t h", t=NT)
                nc.vector.reciprocal(rd, src[:, :, :, HD]).then_inc(rden_done[h], 1)
                wait(dve, rden_done[h], i + 1)
                nc.vector.tensor_tensor(
                    On[:, :, h * 64:(h + 1) * 64].rearrange("p t (h d) -> p t h d", d=HD), src[:, :, :, 0:HD],
                    rden[h][:, :].rearrange("p (t h a) -> p t h a", t=NT, a=1).broadcast_to([128, NT, HALF, HD]),
                    ALU.mult).then_inc(dt_taken[h], 1)

            def residual(i):
                wait(dve, wf_done, i + 1)
                nc.vector.scalar_tensor_tensor(out=x1[:, bass.ds(i * SEQ, SEQ)], in0=M_ps[0][:, 0:SEQ],
                                               scalar=A("bf"), in1=xT[:, bass.ds(i * SEQ, SEQ)],
                                               op0=ALU.add, op1=ALU.add).then_inc(x1_done, 1)

            def step(i, p, ahead, now, finish):
                for g in range(4):
                    for c in range(3):
                        if ahead:
                            reduce_chunk(i + 1, 1 - p, g, c)
                        if now and (g, c) == (0, 0):
                            split_max(i, 1)
                        if isinstance(i, int) and i == 0 and (g, c) == (0, 1):
                            low_part(B - 1, (B - 1) % 2)
                        if ahead and (g, c) == (2, 1):
                            split_max(i + 1, 0)
                    if finish and g == 1:
                        normalise(i - 1, 0)
                        normalise(i - 1, 1)
                if finish:
                    residual(i - 1)

            def reduce_first_batch(k, c):
                if S0_AT <= k < S0_AT + 4:
                    reduce_chunk(0, 0, k - S0_AT, c)

            for k in range(B + 1):
                if k == 3:
                    weigh_lora()
                if k < B:
                    half_up(k, k % 2)
                reduce_first_batch(k, 0)
                if k < B:
                    hide(k, k % 2)
                if k == 0:
                    dve.wait_ge(pa_in, 16)
                    nc.vector.tensor_scalar(bq_scaled[:, :], A("bq"), SCALE, None, ALU.mult).then_inc(bq_done, 1)
                reduce_first_batch(k, 1)
                if k == S0_AT + 2:
                    split_max(0, 0)
                if k >= 2:
                    low_part(k - 2, k % 2)
                if 1 <= k <= B:
                    take_v(k - 1, (k - 1) % 2)
                reduce_first_batch(k, 2)
            step(0, 0, True, True, False)
            with dve.Fori(0, 3) as t:
                step(2 * t + 1, 1, True, True, True)
                step(2 * t + 2, 0, True, True, True)

            def split_p(rows, n):
                dve.wait_ge(p_done, n + 1)
                nc.vector.tensor_scalar(P32[rows, :], S_ps[0][rows, :], pbias[rows, 0:1], None, ALU.add)\
                    .then_inc(p32_done, 1)
                dve.wait_ge(p32_done, n + 1)
                nc.vector.tensor_copy(Pparts[rows, 0, :], P32[rows, :]).then_inc(pchain, 1)
                dve.wait_ge(pchain, 4 * n + 1)
                nc.vector.tensor_tensor(Prest[rows, :], P32[rows, :], Pparts[rows, 0, :], ALU.subtract)\
                    .then_inc(pchain, 1)
                dve.wait_ge(pchain, 4 * n + 2)
                nc.vector.tensor_copy(Pparts[rows, 1, :], Prest[rows, :]).then_inc(pchain, 1)
                dve.wait_ge(pchain, 4 * n + 3)
                nc.vector.tensor_tensor(Pparts[rows, 2, :], Prest[rows, :], Pparts[rows, 1, :], ALU.subtract)\
                    .then_inc(pchain, 1)

            def stack_p(j):
                dve.wait_ge(pchain, 4 * max(j, 1))
                for s, part in enumerate((0, 1, 2, 0)):
                    last = nc.vector.tensor_copy(Pstack[j][32 * s:32 * s + 32, :], Pparts[32 * j:32 * j + 32, part, :])
                last.then_inc(stack_done, 1)

            def take_q(j):
                dve.wait_ge(q_done, j + 1)
                if j >= 2:
                    dve.wait_ge(y_done, j - 1)
                nc.vector.tensor_copy(Q4[j % 2][:, :], O_ps[j % 2][:, :]).then_inc(q_taken, 1)

            def finish(j):
                dve.wait_ge(y_done, j + 1)
                if j >= 2:
                    dve.wait_ge(out_done[j % 2], 16)
                nc.vector.scalar_tensor_tensor(
                    out=Y[j % 2][:, :].rearrange("p (q s) -> p q s", q=2),
                    in0=M_ps[1 - j % 2][:, :].rearrange("p (q s) -> p q s", q=2), scalar=F("b2"),
                    in1=x1[:, :].rearrange("p (q j s) -> p q j s", q=2, j=4)[:, :, j, :],
                    op0=ALU.add, op1=ALU.add).then_inc(y_taken, 1)

            split_max(7, 1)
            stack_v1()
            split_p(slice(0, 64), 0)
            normalise(6, 0)
            normalise(6, 1)
            stack_p(0)
            residual(6)
            stack_p(1)
            split_p(slice(64, 96), 1)
            normalise(7, 0)
            normalise(7, 1)
            stack_p(2)
            take_q(0)
            residual(7)
            split_p(slice(96, 128), 2)
            stack_p(3)
            take_q(1)
            finish(0)
            take_q(2)
            finish(1)
            finish(2)
            take_q(3)
            finish(3)

        @block.tensor
        def _(pe):
            def up(b, p):
                pe.wait_ge(w_in[b], 16)
                if b in (0, 1, 4):
                    pe.wait_ge(x_in[(0, 1, 4).index(b)], 16)
                wait(pe, half_done, 2 * (b - 1))
                for h in range(HC):
                    last = nc.tensor.matmul(up_ps[p][:, h * SEQ:(h + 1) * SEQ],
                                            wexp[b][:, WU0 + h * 128:WU0 + (h + 1) * 128],
                                            xT[:, b * SEQ:(b + 1) * SEQ], start=True, stop=True)
                last.then_inc(up_done, 1)

            def gate(b, p):
                if b == 0:
                    pe.wait_ge(w_rest_in, 16)
                wait(pe, hid_done, b)
                for h in range(HC):
                    last = nc.tensor.matmul(gate_ps[:, h * SEQ:(h + 1) * SEQ],
                                            wexp[b][:, WG0 + h * 128:WG0 + (h + 1) * 128],
                                            xT[:, b * SEQ:(b + 1) * SEQ], start=True, stop=True)
                last.then_inc(gate_done, 1)

            def down(b, p):
                pe.wait_ge(hid_done, b + 1)
                wait(pe, c_taken, b)
                for h in range(HC):
                    last = nc.tensor.matmul(c_ps[:, 0:SEQ], wexp[b][:, WD0 + h * 128:WD0 + (h + 1) * 128],
                                            hidden[p][:, h * SEQ:(h + 1) * SEQ], start=(h == 0), stop=(h == HC - 1))
                last.then_inc(down_done, 1)

            def project(b, p):
                if b == 0:
                    pe.wait_ge(pa_in, 16)
                pe.wait_ge(c_taken, b + 1)
                wait(pe, qk32_done, 2 * b)
                nc.tensor.matmul(qk_ps[:, 0:SEQ], A("wq"), cT[p][:, :], start=True, stop=True)
                nc.tensor.matmul(qk_ps[:, SEQ:2 * SEQ], A("wk"), cT[p][:, :], start=True, stop=True)\
                    .then_inc(qkmm_done, 1)
                wait(pe, v_taken, b)
                if b == S0_AT + 1:
                    pe.wait_ge(mt_taken[0], 1)
                for t in range(NT):
                    last = nc.tensor.matmul(v_ps[:, t * D:(t + 1) * D], cT[p][:, t * 128:(t + 1) * 128], A("wv"),
                                            start=True, stop=True)
                last.then_inc(vmm_done, 1)

            def fold_lora():
                pe.wait_ge(pf_in, 16)
                nc.tensor.matmul(S_ps[0][:, 0:RANK], F("lora_b"), F("u1")[:, 0:RANK], start=True, stop=True)\
                    .then_inc(lm_done, 1)

            def fold_base():
                pe.wait_ge(lw_done, 1)
                nc.tensor.matmul(S_ps[1][:, 0:B * RANK], F("lora_a"), lora_w[:, :], start=True, stop=False)
                nc.tensor.matmul(S_ps[1][:, 0:B * RANK], F("base"), F("u1"), start=False, stop=True).then_inc(g_done, 1)
                pe.wait_ge(lm_taken, 1)
                nc.tensor.matmul(S_ps[0][:, 64:65], F("u1")[:, 0:128], F("b_base"), start=True, stop=True)\
                    .then_inc(g_done, 1)

            def scores(side, ps, stationary, moving, rows, g, c):
                part, full, pair, mask = chunk_kind(side, g // 2, c)
                nh = 2 if full else 4
                view = ps[:, :].rearrange("p (h s) -> p h s", h=nh)
                diag = view[:, :, part * 128:(part + 1) * 128] if full else view
                nc.tensor.matmul(diag, ident_b, mask.rearrange("p (a s) -> p a s", a=1).broadcast_to([128, nh, 128]),
                                 start=True, stop=False, skip_group_check=True)
                for n in range(nh):
                    head = 4 * g + (2 * pair if full else 0) + n
                    rhs = moving[0:rows, head, :] if full else moving[0:rows, head, part * 128:(part + 1) * 128]
                    last = nc.tensor.matmul(view[:, n, :], stationary[0:rows, head, part * 128:(part + 1) * 128], rhs,
                                            start=False, stop=(n == nh - 1), skip_group_check=True)
                return last

            def s_chunk(i, p, g, c, count):
                n = 3 * g + c
                if n in (0, 6):
                    pe.wait_ge(qk_in[n // 6][p], 32 * count)
                wait(pe, max_done, CH * i + n - 1)
                scores("S", S_ps[n % 2], QS[p], KS[p], R_MAXROW, g, c).then_inc(s_done, 1)

            def s_first_batch(k, c):
                if S0_AT <= k < S0_AT + 4:
                    s_chunk(0, 0, k - S0_AT, c, 1)

            def s_first():
                pe.wait_ge(g_taken, 1)
                pe.wait_ge(pb_done, 1)
                pe.wait_ge(cb_in, 16)
                pe.wait_ge(const_in, 64)

            def t_chunk(i, p, g, c):
                n = 3 * g + c
                if n in (0, 6):
                    wait(pe, mrow_in[n // 6], 32 * (i + 1))
                wait(pe, exp_done, CH * i + n - 1)
                scores("T", T_ps[n % 2], KS[p], QS[p], R_ALL, g, c).then_inc(t_done, 1)

            def pv(i, p, g):
                h = g // 2
                if g == 0:
                    wait(pe, va_done, i + 1)
                if g % 2 == 0:
                    wait(pe, o_taken[h], i)
                wait(pe, exp_done, CH * i + 3 * g + 3)
                cols = (g % 2) * SEQ
                for c, part in ((0, h), (2, 1 - h)):
                    for j in range(4):
                        v = vaug[p][:, part, 4 * g + j, :]
                        if c == 0:
                            last = nc.tensor.matmul(O_ps[h][32 * j:32 * j + 32, cols:cols + SEQ], v,
                                                    PB[g][j // 2][:, (j % 2) * SEQ:(j % 2 + 1) * SEQ],
                                                    start=(g % 2 == 0), stop=False, skip_group_check=True)
                        else:
                            at = cols + part * 128
                            last = nc.tensor.matmul(O_ps[h][32 * j:32 * j + 32, at:at + 128], v,
                                                    PB[g][2][:, j * 128:(j + 1) * 128],
                                                    start=False, stop=True, skip_group_check=True)
                last.then_inc(pv_done, 1)

            def turn_max(i, p, h):
                wait(pe, max_done, CH * i + 6 * (h + 1))
                if h == 1:
                    wait(pe, mt_taken[0], i + 1)
                    if isinstance(i, int) and i == 0:
                        pe.wait_ge(v_taken, B)
                else:
                    wait(pe, dt_taken[1], i - 1)
                nc.tensor.transpose(turned_max, mx[p][:, h * HALF * NT:(h + 1) * HALF * NT], A("ident"))\
                    .then_inc(mt_done[h], 1)

            def turn_o(i, h):
                wait(pe, o_taken[h], i + 1)
                if h == 0:
                    wait(pe, x1_done, i)
                else:
                    wait(pe, mt_taken[1], min(i + 2, B) if isinstance(i, int) else i + 2)
                for t in range(NT):
                    for g in range(2):
                        at = g * SEQ + t * 128
                        last = nc.tensor.transpose(M_ps[h][:, t * 256 + g * 128:t * 256 + (g + 1) * 128],
                                                   OS[h][:, at:at + 128], A("ident"))
                last.then_inc(dt_done[h], 1)

            def turn_on(i):
                for h in range(2):
                    wait(pe, dt_taken[h], i + 1)
                for t in range(NT):
                    last = nc.tensor.transpose(M_ps[0][:, t * 128:(t + 1) * 128], On[:, t, :], A("ident"))
                last.then_inc(ont_done, 1)

            def out_project(i):
                wait(pe, ont_taken, i + 1)
                nc.tensor.matmul(M_ps[0][:, 0:SEQ], A("wf"), OnT[:, :], start=True, stop=True).then_inc(wf_done, 1)

            def step(i, p, count, ahead, now, finish):
                for g in range(4):
                    for c in range(3):
                        if ahead:
                            s_chunk(i + 1, 1 - p, g, c, count)
                        if now:
                            t_chunk(i, p, g, c)
                        if now and (g, c) == (0, 0):
                            turn_max(i, p, 1)
                        if ahead and (g, c) == (2, 1):
                            turn_max(i + 1, 1 - p, 0)
                    if finish and g == 0:
                        pv(i - 1, 1 - p, 3)
                    if now and g >= 1:
                        pv(i, p, g - 1)
                    if finish and g == 1:
                        turn_o(i - 1, 0)
                        turn_o(i - 1, 1)
                    if finish and g == 2:
                        turn_on(i - 1)
                if finish:
                    out_project(i - 1)

            for k in range(B + 1):
                if k < B:
                    up(k, k % 2)
                if k == S0_AT:
                    s_first()
                s_first_batch(k, 0)
                if k >= 1:
                    down(k - 1, (k - 1) % 2)
                if k < B:
                    gate(k, k % 2)
                s_first_batch(k, 1)
                if k == S0_AT + 2:
                    pe.wait_ge(v_taken, k - 1)
                    turn_max(0, 0, 0)
                if k >= 1:
                    project(k - 1, (k - 1) % 2)
                s_first_batch(k, 2)
                if k == 2:
                    fold_lora()
                if k == 3:
                    fold_base()
            step(0, 0, 1, True, True, False)
            pe.wait_ge(qk32_done, 2 * B)
            with pe.Fori(0, 3) as t:
                step(2 * t + 1, 1, t + 2, True, True, True)
                step(2 * t + 2, 0, t + 2, True, True, True)

            def low_rank(b):
                j, q = b % 4, b // 4
                return nc.tensor.matmul(S_ps[0][32 * j:32 * j + 32, q * SEQ:(q + 1) * SEQ],
                                        G[:, b * RANK:(b + 1) * RANK], x1[:, b * SEQ:(b + 1) * SEQ],
                                        start=(q == 0), stop=True, skip_group_check=True)

            def ff_up(j, f0, f1):
                pe.wait_ge(stack_done, j + 1)
                for f in range(f0, f1):
                    n = NF * j + f
                    if n >= 3:
                        pe.wait_ge(gelu_done, n - 2)
                    for w in (v1_first, v1_second):
                        last = nc.tensor.matmul(bank[1 + n % 3][:, :], w[:, f * 128:(f + 1) * 128], Pstack[j][:, :],
                                                start=(w is v1_first), stop=(w is v1_second))
                    last.then_inc(h_done, 1)

            def ff_rank(j):
                pe.wait_ge(gelu_done, NF * (j + 1))
                if j >= 2:
                    pe.wait_ge(q_taken, j - 1)
                for f in range(NF):
                    last = nc.tensor.matmul(O_ps[j % 2][32 * f:32 * f + 32, :], u2[:, f, :], H[j % 2][f],
                                            start=True, stop=True)
                last.then_inc(q_done, 1)

            def ff_down(j):
                pe.wait_ge(q_taken, j + 1)
                if j >= 2:
                    pe.wait_ge(y_taken, j - 1)
                nc.tensor.matmul(M_ps[1 - j % 2][:, :], F("v2"), Q4[j % 2][:, :], start=True, stop=True)\
                    .then_inc(y_done, 1)

            pe.wait_ge(max_done, CH * B)
            pe.wait_ge(x1_done, 6)
            for g in range(4):
                for c in range(3):
                    t_chunk(7, 1, g, c)
                    if (g, c) == (0, 0):
                        turn_max(7, 1, 1)
                if g == 0:
                    pv(6, 0, 3)
                    for b in range(6):
                        last = low_rank(b)
                    last.then_inc(p_done, 1)
                else:
                    pv(7, 1, g - 1)
                if g == 1:
                    turn_o(6, 0)
                    turn_o(6, 1)
                if g == 2:
                    turn_on(6)
            out_project(6)
            pv(7, 1, 3)
            pe.wait_ge(x1_done, 7)
            pe.wait_ge(p32_done, 1)
            low_rank(6).then_inc(p_done, 1)
            pe.wait_ge(exp_done, CH * B)
            pe.wait_ge(v1_stacked, 1)
            ff_up(0, 0, NF)
            turn_o(7, 0)
            turn_o(7, 1)
            ff_up(1, 0, 3)
            turn_on(7)
            ff_up(1, 3, NF)
            pe.wait_ge(o_taken[0], B)
            ff_rank(0)
            out_project(7)
            ff_up(2, 0, 2)
            pe.wait_ge(x1_done, B)
            pe.wait_ge(p32_done, 2)
            low_rank(7).then_inc(p_done, 1)
            ff_up(2, 2, NF)
            pe.wait_ge(o_taken[1], B)
            ff_rank(1)
            ff_down(0)
            ff_rank(2)
            ff_up(3, 0, NF)
            ff_down(1)
            ff_down(2)
            ff_rank(3)
            ff_down(3)


def _packed(inputs):
    import numpy as np

    f32 = np.float32
    g = {k: np.asarray(v) for k, v in inputs.items()}
    xT = np.ascontiguousarray(g["x"].reshape(B * SEQ, D).T)

    def hidden_bias(v):
        return v.reshape(EXPERTS, HC, 128).transpose(0, 2, 1)

    wexp = np.concatenate([
        hidden_bias(g["L0_cond_b_up"]), hidden_bias(g["L0_cond_b_gate"]), g["L0_cond_b_down"][:, :, None],
        g["L0_cond_W_up"].transpose(0, 2, 1), g["L0_cond_W_gate"].transpose(0, 2, 1),
        g["L0_cond_W_down"].reshape(EXPERTS, D, HC, 128).transpose(0, 3, 2, 1).reshape(EXPERTS, 128, HC * D)], axis=2)

    def by_d(w):
        return w.reshape(w.shape[:-1] + (HEADS, HD)).swapaxes(-1, -2).reshape(w.shape)

    pa = np.concatenate([
        by_d(g["L0_attn_Wq"]), by_d(g["L0_attn_Wk"]), g["L0_attn_Wv"], g["L0_attn_Wf"], np.eye(128, dtype=f32),
        np.tile(g["L0_attn_bv"][None], (128, 1)), by_d(g["L0_attn_bq"])[:, None], by_d(g["L0_attn_bk"])[:, None],
        g["L0_attn_bf"][:, None]], axis=1)

    pf = np.concatenate([
        g["L0_cond2_W_base"], g["L0_cond2_Bs"].transpose(1, 0, 2).reshape(D, EXPERTS * RANK_L),
        g["L0_cond2_As"].reshape(EXPERTS * RANK_L, D), np.tile(g["L0_ffn_U1"], (1, B)),
        g["L0_cond2_b_base"][:, None], np.repeat(g["cond_8"].T, RANK_L, axis=0), g["L0_ffn_b1"].reshape(NF, 128).T,
        g["L0_ffn_U2"].reshape(NF, 128, RANK).transpose(1, 0, 2).reshape(128, NF * RANK),
        np.tile(g["L0_ffn_V2"], (NF, 1)), g["L0_ffn_b2"][:, None], np.tile(g["L0_ffn_V1"], (4, 1))], axis=1)

    bf = np.dtype("bfloat16")
    neg = f32(-1e9)
    tri = np.arange(128)
    cb = np.concatenate([np.eye(128, dtype=f32), np.where(tri[None] > tri[:, None], neg, f32(0)),
                         np.where(tri[None] < tri[:, None], neg, f32(0))], axis=1).astype(bf)

    base = 24.0 ** (1.0 / HALF)
    slope = (f32(1.0) / f32(base) ** np.arange(1, HALF + 1, dtype=f32)).astype(f32)
    signed = np.concatenate([slope, -slope])
    three = []
    left = signed.copy()
    for _ in range(3):
        three.append(left.astype(bf).astype(f32))
        left = left - three[-1]
    pos = np.arange(SEQ, dtype=f32)
    qc = np.zeros((R_CONST, HEADS, SEQ), f32)
    kc = np.zeros((R_CONST, HEADS, SEQ), f32)
    for n, s in enumerate(three):
        qc[n], kc[n] = s[:, None], pos[None]
        qc[3 + n], kc[3 + n] = -pos[None], s[:, None]
    kc[R_MAXROW - R_STACK:] = 1.0
    return [xT, wexp, g["cond_8"], pa, pf, cb, qc.astype(bf), kc.astype(bf)]


_INS = ["xT", "wexp", "cond", "pa", "pf", "cb", "qc", "kc"]


def kernel(**inputs):
    import numpy as _np
    import concourse.bacc as _bacc
    from concourse import mybir as _mybir
    from concourse.bass_utils import run_bass_kernel_spmd as _run

    nc = _bacc.Bacc("TRN2", target_bir_lowering=False, num_devices=1)
    arrays, args = {}, []
    for name, a in zip(_INS, _packed(inputs)):
        a = _np.ascontiguousarray(a)
        arrays[f"in_{name}_dram"] = a
        args.append(nc.dram_tensor(f"in_{name}_dram", a.shape, _mybir.dt.from_np(a.dtype), kind="ExternalInput").ap())
    args.append(nc.dram_tensor("out_0_dram", (D, B * SEQ), _mybir.dt.float32, kind="ExternalOutput").ap())
    adaln_attention_ffn(nc, *args)
    r = _run(nc, [arrays], core_ids=[0])
    got = r.results[0]["out_0_dram"]
    return _np.ascontiguousarray(_np.asarray(got).T).reshape(B, SEQ, D)
```

```python
import concourse.bass as bass
from concourse import mybir
from contextlib import ExitStack

B, SEQ, D = 8, 256, 128
HEADS, HD = 16, 8
HALF = HEADS // 2
EXPERTS, RANK_L = 8, 16
FF, RANK = 512, 32
NF = FF // 128
HC = 2
NT = SEQ // 128
SCALE = 1.0 / HD ** 0.5
LORA_SCALE = 32.0 / RANK_L

BU0, BG0, BD0, WU0 = 0, HC, 2 * HC, 2 * HC + 1
WG0, WD0, WCOLS = WU0 + HC * 128, WU0 + 2 * HC * 128, WU0 + 3 * HC * 128

A_COLS = {}
_at = 0
for _n, _w in (("wq", 128), ("wk", 128), ("wv", 128), ("wf", 128), ("ident", 128), ("bv", 128),
               ("bq", 1), ("bk", 1), ("bf", 1)):
    A_COLS[_n] = (_at, _at + _w)
    _at += _w
A_TOTAL = _at

F_COLS = {}
_at = 0
for _n, _w in (("base", 128), ("lora_b", 128), ("lora_a", 128), ("u1", 8 * RANK), ("b_base", 1), ("cond", B),
               ("b1", NF), ("u2", NF * RANK), ("v2", 128), ("b2", 1), ("v1", FF)):
    F_COLS[_n] = (_at, _at + _w)
    _at += _w
F_TOTAL = _at

PARTS = 3
STAGES = 4
R_STACK = PARTS * PARTS * HD
R_MAXROW = R_STACK + 2 * PARTS
R_ALL = R_MAXROW + 2
R_CONST = R_ALL - R_STACK
CH = 12
UNITS = ((0, 0, 2 * SEQ), (1, 0, 2 * SEQ), (3, 0, SEQ), (2, 0, 2 * SEQ), (3, SEQ, 2 * SEQ))
S0_PLACE = 15
MAX_AT = (S0_PLACE + 7) // 3


def adaln_attention_ffn(nc, xT_d, wexp_d, cond_d, pa_d, pf_d, cb_d, qc_d, kc_d, out_d):
    fp32, bf16, u32 = mybir.dt.float32, mybir.dt.bfloat16, mybir.dt.uint32
    ALU, ACT, AX = mybir.AluOpType, mybir.ActivationFunctionType, mybir.AxisListType

    stage_qk = nc.dram_tensor("stage_qk", [B, 2, PARTS, 128, SEQ], bf16, kind="Internal").ap()
    stage_v = nc.dram_tensor("stage_v", [B, 128, NT * D], fp32, kind="Internal").ap()

    ctx = ExitStack()
    with ctx:
        def sb(name, shape, dt=fp32):
            return ctx.enter_context(nc.sbuf_tensor(name, shape, dt))

        def sem(name):
            return ctx.enter_context(nc.semaphore(name))

        xT = sb("xT", [128, B * SEQ])
        x1 = sb("x1", [128, B * SEQ])
        pa = sb("pa", [128, A_TOTAL])
        pf = sb("pf", [128, F_TOTAL])
        cb = sb("cb", [128, 3 * 128], bf16)
        ident_b, mask_up, mask_lo = cb[:, 0:128], cb[:, 128:256], cb[:, 256:384]
        cond_sb = sb("cond_sb", [B, EXPERTS])
        top = sb("top", [B, 8])
        expert = sb("expert", [B, 8], u32)
        wexp = [sb(f"wexp{b}", [128, WCOLS]) for b in range(B)]
        bq_scaled = sb("bq_scaled", [128, 1])
        sig_up = [sb(f"sig_up{p}", [128, 512]) for p in range(2)]
        silu_up = [sb(f"silu_up{p}", [128, 512]) for p in range(2)]
        hidden = [sb(f"hidden{p}", [128, 512]) for p in range(2)]
        cT = [sb(f"cT{p}", [128, SEQ]) for p in range(2)]
        qk32 = [sb(f"qk32{p}", [128, 2 * SEQ]) for p in range(2)]
        rest = [sb(f"rest{p}", [128, 2 * SEQ]) for p in range(2)]
        parts = [sb(f"parts{p}", [128, 2, PARTS, SEQ], bf16) for p in range(STAGES)]
        vrow = [sb(f"vrow{p}", [128, NT * D]) for p in range(STAGES)]
        QS = [sb(f"QS{p}", [R_ALL, HEADS, SEQ], bf16) for p in range(2)]
        KS = [sb(f"KS{p}", [R_ALL, HEADS, SEQ], bf16) for p in range(2)]
        vload = [sb(f"vload{p}", [128, NT * D]) for p in range(2)]
        vaug = [sb(f"vaug{p}", [128, NT, HEADS, 32]) for p in range(2)]
        mx = [sb(f"mx{p}", [128, HEADS * NT]) for p in range(2)]
        mrow = [sb(f"mrow{h}", [HALF * NT, 2, 128], bf16) for h in range(2)]
        PB = [[sb(f"PB{g}{c}", [128, 512]) for c in range(3)] for g in range(4)]
        OS = [sb(f"OS{h}", [128, SEQ]) for h in range(2)]
        rden = [sb(f"rden{h}", [128, NT * HALF]) for h in range(2)]
        On = sb("On", [128, NT, D])
        OnT = sb("OnT", [128, SEQ])
        lora_m = sb("lora_m", [128, RANK])
        lora_w = sb("lora_w", [128, B * RANK])
        G = sb("G", [128, B * RANK])
        pbias = sb("pbias", [128, 1])
        warm = sb("warm", [128, 1])
        Prest = sb("Prest", [128, 512])
        Pparts = sb("Pparts", [128, 3, 512], bf16)
        Pstack = [sb(f"Pstack{j}", [128, 512], bf16) for j in range(4)]
        v1_parts = sb("v1_parts", [128, 3, FF], bf16)
        v1_rest = sb("v1_rest", [128, FF])
        v1_first = sb("v1_first", [128, FF], bf16)
        v1_second = sb("v1_second", [128, FF], bf16)
        H = [[wexp[NF * p + f][:, 0:512] for f in range(NF)] for p in range(2)]
        Q4 = [sb(f"Q4{j}", [128, 512]) for j in range(2)]
        Y = [sb(f"Y{j}", [128, 512]) for j in range(2)]

        bank = [ctx.enter_context(nc.psum_tensor(f"bank{n}", [128, 512], fp32)) for n in range(8)]
        up_ps = bank[2:4]
        gate_ps, c_ps, qk_ps, v_ps = bank[4:8]
        S_ps, T_ps, O_ps, M_ps = bank[0:2], bank[2:4], bank[4:6], bank[6:8]

        last_ps = (bank[2], bank[3], bank[1])
        turned_max = M_ps[1][0:HALF * NT, 0:128]

        def slot_view(v, a):
            return v.rearrange("p t (h a j) r -> p (t h) a j r", a=2, j=4)[:, :, a, :, :]

        def A(name):
            return pa[:, A_COLS[name][0]:A_COLS[name][1]]

        def F(name):
            return pf[:, F_COLS[name][0]:F_COLS[name][1]]

        u2 = F("u2").rearrange("p (f r) -> p f r", f=NF)

        cond_in, pa_in, pf_in, cb_in, const_in = map(sem, ("cond_in", "pa_in", "pf_in", "cb_in", "const_in"))
        x_in = [sem(f"x_in{n}") for n in range(2)]
        w_in = [sem(f"w_in{b}") for b in range(B)]
        w_rest_in = sem("w_rest_in")
        staged = [sem(f"staged{p}") for p in range(STAGES)]
        qk_in = [[sem(f"qk_in{h}{p}") for p in range(2)] for h in range(2)]
        v_in = [sem(f"v_in{p}") for p in range(2)]
        mrow_in = [sem(f"mrow_in{h}") for h in range(2)]
        top_done, expert_done = sem("top_done"), sem("expert_done")
        up_done, gate_done, sig_done, silu_done, hid_done, down_done, c_taken = map(
            sem, ("up_done", "gate_done", "sig_done", "silu_done", "hid_done", "down_done", "c_taken"))
        qkmm_done, vmm_done, qk32_done, v_taken, hi_done, rest_done, mid_done, low_done = map(
            sem, ("qkmm_done", "vmm_done", "qk32_done", "v_taken", "hi_done", "rest_done", "mid_done", "low_done"))
        zero_done, bq_done, v1_done, v1_stacked = map(sem, ("zero_done", "bq_done", "v1_done", "v1_stacked"))
        lm_done, lm_taken, lw_done, g_done, g_taken, pb_done = map(
            sem, ("lm_done", "lm_taken", "lw_done", "g_done", "g_taken", "pb_done"))
        s_done, max_done, t_done, exp_done, pv_done, va_done = map(
            sem, ("s_done", "max_done", "t_done", "exp_done", "pv_done", "va_done"))
        o_taken = [sem(f"o_taken{h}") for h in range(2)]
        mt_done = [sem(f"mt_done{h}") for h in range(2)]
        mt_hi = [sem(f"mt_hi{h}") for h in range(2)]
        mt_taken = [sem(f"mt_taken{h}") for h in range(2)]
        dt_done = [sem(f"dt_done{h}") for h in range(2)]
        rden_done = [sem(f"rden_done{h}") for h in range(2)]
        dt_taken = [sem(f"dt_taken{h}") for h in range(2)]
        ont_done, ont_taken, wf_done, x1_done = map(sem, ("ont_done", "ont_taken", "wf_done", "x1_done"))
        p_done, p_split, stack_done, h_done, gelu_done, q_done, y_done, y_taken = map(
            sem, ("p_done", "p_split", "stack_done", "h_done", "gelu_done", "q_done", "y_done", "y_taken"))
        q_taken = [sem(f"q_taken{p}") for p in range(2)]
        out_done = [sem(f"out_done{p}") for p in range(2)]

        block = ctx.enter_context(nc.Block())

        def wait(eng, s, value):
            if isinstance(value, int) and value <= 0:
                return
            eng.wait_ge(s, value)

        def chunk_kind(side, half, c):
            full = (c > 0) if side == "S" else (c < 2)
            if side == "S":
                part = (1 if full else 0) if half == 0 else (0 if full else 1)
                mask = mask_up if half == 0 else mask_lo
                pair = c - 1
            else:
                part = (0 if full else 1) if half == 0 else (1 if full else 0)
                mask = mask_lo if half == 0 else mask_up
                pair = c
            return part, full, pair, mask

        @block.sync
        def _(sp):
            sp.dma_start(cond_sb[:, :], cond_d).then_inc(cond_in, 16)
            sp.dma_start(pa[:, :], pa_d).then_inc(pa_in, 16)
            sp.wait_ge(expert_done, 1)
            for b in range(B):
                e = sp.value_load(expert[b:b + 1, 0:1], min_val=0, max_val=EXPERTS - 1)
                for c0, c1 in ((0, WG0), (WG0, WCOLS)) if b == 0 else ((0, WCOLS),):
                    sp.dma_start(wexp[b][:, c0:c1], wexp_d[bass.ds(e, 1), :, c0:c1].rearrange("a p n -> (a p) n"))\
                        .then_inc(w_in[b] if c0 == 0 else w_rest_in, 16)
                if b == 2:
                    sp.dma_start(pf[:, :], pf_d).then_inc(pf_in, 16)
                    sp.dma_start(xT[:, 4 * SEQ:], xT_d[:, 4 * SEQ:]).then_inc(x_in[1], 16)
            sp.dma_start(cb[:, :], cb_d).then_inc(cb_in, 16)
            for p in range(2):
                sp.dma_start(QS[p][R_STACK:R_ALL, :, :], qc_d).then_inc(const_in, 16)
                sp.dma_start(KS[p][R_STACK:R_ALL, :, :], kc_d).then_inc(const_in, 16)

            def store_stage(b):
                sp.wait_ge(low_done, b + 1)
                sp.dma_start(stage_qk[b].rearrange("a j p s -> p (a j) s"),
                             parts[b % STAGES][:, :, :, :].rearrange("p a j s -> p (a j) s"))\
                    .then_inc(staged[b % STAGES], 16)
                sp.wait_ge(v_taken, b + 1)
                sp.dma_start(stage_v[b], vrow[b % STAGES][:, :]).then_inc(staged[b % STAGES], 16)

            def load_half(b, p, h):
                rows = slice(h * HALF, (h + 1) * HALF)
                q, k = (stage_qk[bass.ds(b, 1), n, :, :, :].rearrange("a j (d h) s -> a (j d) h s", d=HD)[:, :, rows, :]
                        for n in range(2))
                sp.dma_start(QS[p][0:R_STACK, rows, :], q.broadcast_to([PARTS, PARTS * HD, HALF, SEQ]))\
                    .then_inc(qk_in[h][p], 16)
                for i in range(PARTS):
                    at = i * PARTS * HD
                    sp.dma_start(KS[p][at:at + PARTS * HD, rows, :],
                                 k[:, i * HD:(i + 1) * HD, :, :].broadcast_to([PARTS, HD, HALF, SEQ]))\
                        .then_inc(qk_in[h][p], 16)

            def load_v(b, p):
                sp.dma_start(vload[p][:, :], stage_v[bass.ds(b, 1)].rearrange("a p n -> (a p) n"))\
                    .then_inc(v_in[p], 16)

            def max_rows(b, p, h):
                wait(sp, mt_taken[h], b + 1)
                for r in range(2):
                    sp.dma_start(QS[p][R_MAXROW + r:R_MAXROW + r + 1, h * HALF:(h + 1) * HALF, :],
                                 mrow[h][:, r, :]).then_inc(mrow_in[h], 16)

            for b in range(B - 1):
                store_stage(b)
                if b < 2:
                    sp.wait_ge(staged[b], 2 * 16)
                    load_half(b, b, 0)
                    load_half(b, b, 1)
                    load_v(b, b)
                if b == MAX_AT - 2:
                    max_rows(0, 0, 0)

            def attention_loads(i, p, last):
                max_rows(i, p, 1)
                if not last:
                    wait(sp, t_done, CH * i + 6)
                    load_half(i + 2, p, 0)
                    wait(sp, va_done, 2 * i + 2)
                    load_v(i + 2, p)

            sp.wait_ge(staged[2], 2 * 16)
            attention_loads(0, 0, False)
            max_rows(1, 1, 0)
            store_stage(B - 1)
            for s in range(STAGES):
                sp.wait_ge(staged[s], 2 * 16 * B // STAGES)
            wait(sp, t_done, CH)
            load_half(2, 0, 1)
            with sp.Fori(0, 2) as t:
                for p in (1, 0):
                    i = 2 * t + (1 if p else 2)
                    attention_loads(i, p, False)
                    max_rows(i + 1, 1 - p, 0)
                    wait(sp, t_done, CH * i + CH)
                    load_half(i + 2, p, 1)
            attention_loads(5, 1, False)
            max_rows(6, 0, 0)
            wait(sp, t_done, CH * 6)
            load_half(7, 1, 1)
            attention_loads(6, 0, True)
            max_rows(7, 1, 0)
            attention_loads(7, 1, True)

            view = out_d.rearrange("p (q j s) -> p q j s", q=2, j=4)
            for u, (j, c0, c1) in enumerate(UNITS):
                sp.wait_ge(y_taken, u + 1)
                sp.dma_start(view[:, c0 // SEQ:c1 // SEQ, j, :],
                             Y[u % 2][:, 0:c1 - c0].rearrange("p (q s) -> p q s", s=SEQ)).then_inc(out_done[u % 2], 16)
            for p in range(2):
                sp.wait_ge(out_done[p], 16 * len(UNITS[p::2]))

        @block.gpsimd
        def _(pool):
            pool.memset(v1_second[:, :], 0.0).then_inc(zero_done, 1)
            for p in range(2):
                pool.memset(vaug[p][:, :, :, :], 0.0).then_inc(zero_done, 1)
            pool.wait_ge(zero_done, 3)
            for p in range(2):
                for a in range(2):
                    pool.memset(slot_view(vaug[p][:, :, :, :], a)[:, :, :, 16 + HD * a:17 + HD * a], 1.0)\
                        .then_inc(zero_done, 1)

            def remainder(b, p):
                pool.wait_ge(hi_done, b + 1)
                pool.tensor_tensor(rest[p][:, :].rearrange("p (a s) -> p a s", a=2),
                                   qk32[p][:, :].rearrange("p (a s) -> p a s", a=2),
                                   parts[b % STAGES][:, :, 0, :], ALU.subtract).then_inc(rest_done, 1)

            def low_part(b, p):
                pool.wait_ge(mid_done, b + 1)
                pool.tensor_tensor(parts[b % STAGES][:, :, 2, :], rest[p][:, :].rearrange("p (a s) -> p a s", a=2),
                                        parts[b % STAGES][:, :, 1, :], ALU.subtract).then_inc(low_done, 1)

            def spread_v(b, p):
                pool.wait_ge(v_in[p], 16 * (b // 2 + 1))
                wait(pool, pv_done, 4 * b - 4)
                src = vload[p][:, :].rearrange("p (t a j d) -> p t a j d", a=2, j=4, d=HD)
                for a in range(2):
                    pool.tensor_copy(slot_view(vaug[p][:, :, :, :], a)[:, :, :, HD * a:HD * (a + 1)],
                                     src[:, :, a, :, :]).then_inc(va_done, 1)

            def split_v1():
                pool.wait_ge(pf_in, 16)
                pool.tensor_copy(v1_parts[:, 0, :], F("v1")).then_inc(v1_done, 1)
                pool.wait_ge(v1_done, 1)
                pool.tensor_tensor(v1_rest[:, :], F("v1"), v1_parts[:, 0, :], ALU.subtract).then_inc(v1_done, 1)
                pool.wait_ge(v1_done, 2)
                pool.tensor_copy(v1_parts[:, 1, :], v1_rest[:, :]).then_inc(v1_done, 1)
                pool.wait_ge(v1_done, 3)
                pool.tensor_tensor(v1_parts[:, 2, :], v1_rest[:, :], v1_parts[:, 1, :], ALU.subtract)\
                    .then_inc(v1_done, 1)

            for b in range(B):
                remainder(b, b % 2)
                low_part(b, b % 2)
            spread_v(0, 0)
            spread_v(1, 1)
            split_v1()

            for b in range(2, B):
                spread_v(b, b % 2)

        @block.scalar
        def _(act):
            act.dma_start(xT[:, 0:4 * SEQ], xT_d[:, 0:4 * SEQ]).then_inc(x_in[0], 16)

            def sigmoid_up(b, p):
                act.wait_ge(up_done, b + 1)
                for h in range(HC):
                    cols = slice(h * SEQ, (h + 1) * SEQ)
                    nc.scalar.activation(sig_up[p][:, cols], up_ps[p][:, cols], ACT.Sigmoid,
                                         bias=wexp[b][:, BU0 + h:BU0 + h + 1]).then_inc(sig_done, 1)

            def take_c(b, p):
                act.wait_ge(down_done, b + 1)
                nc.scalar.activation(cT[p][:, :], c_ps[:, 0:SEQ], ACT.Identity, bias=wexp[b][:, BD0:BD0 + 1])\
                    .then_inc(c_taken, 1)

            def take_qk(b, p):
                act.wait_ge(qkmm_done, b + 1)
                wait(act, rest_done, b - 1)
                nc.scalar.activation(qk32[p][:, 0:SEQ], qk_ps[:, 0:SEQ], ACT.Identity, bias=bq_scaled[:, 0:1],
                                     scale=SCALE).then_inc(qk32_done, 1)
                nc.scalar.activation(qk32[p][:, SEQ:2 * SEQ], qk_ps[:, SEQ:2 * SEQ], ACT.Identity, bias=A("bk"))\
                    .then_inc(qk32_done, 1)

            def high_part(b, p):
                act.wait_ge(qk32_done, 2 * b + 2)
                wait(act, staged[b % STAGES], 2 * 16 * (b // STAGES))
                nc.scalar.activation(parts[b % STAGES][:, :, 0, :], qk32[p][:, :].rearrange("p (a s) -> p a s", a=2),
                                     ACT.Copy).then_inc(hi_done, 1)

            def mid_part(b, p):
                act.wait_ge(rest_done, b + 1)
                nc.scalar.activation(parts[b % STAGES][:, :, 1, :], rest[p][:, :].rearrange("p (a s) -> p a s", a=2),
                                     ACT.Copy).then_inc(mid_done, 1)

            def fold_lora():
                act.wait_ge(lm_done, 1)
                nc.scalar.activation(lora_m[:, :], S_ps[0][:, 0:RANK], ACT.Copy, scale=LORA_SCALE)\
                    .then_inc(lm_taken, 1)

            def fold_base():
                act.wait_ge(g_done, 2)
                nc.scalar.activation(G[:, :], S_ps[1][:, 0:B * RANK], ACT.Copy).then_inc(g_taken, 1)
                nc.scalar.activation(pbias[:, :], S_ps[0][:, 64:65], ACT.Copy).then_inc(pb_done, 1)

            for k in range(B + 1):
                if k < B:
                    sigmoid_up(k, k % 2)
                if k == 2:
                    fold_lora()
                if k == 3:
                    fold_base()
                if k == B - 1:
                    act.wait_ge(pb_done, 1)
                    nc.scalar.activation(warm[:, :], pbias[:, :], ACT.Exp)
                if 1 <= k <= B:
                    take_c(k - 1, (k - 1) % 2)
                if k >= 2:
                    mid_part(k - 2, k % 2)
                if k == 1:
                    act.wait_ge(bq_done, 1)
                if 1 <= k <= B:
                    take_qk(k - 1, (k - 1) % 2)
                    high_part(k - 1, (k - 1) % 2)

            def exp_chunk(i, g, c):
                wait(act, t_done, CH * i + 3 * g + c + 1)
                if c == 0:
                    wait(act, pv_done, 4 * i + g - 3)
                n = 3 * g + c
                src = last_ps[n % 3] if isinstance(i, int) and i == B - 1 else T_ps[n % 2]
                nc.scalar.activation(PB[g][c][:, :], src[:, :], ACT.Exp).then_inc(exp_done, 1)

            def take_o(i, h):
                wait(act, pv_done, 4 * i + 2 * h + 2)
                nc.scalar.activation(OS[h][:, :], O_ps[h][:, 0:SEQ], ACT.Copy).then_inc(o_taken[h], 1)

            def take_ont(i):
                wait(act, ont_done, i + 1)
                nc.scalar.activation(OnT[:, :], M_ps[0][:, 0:SEQ], ACT.Copy).then_inc(ont_taken, 1)

            def step(i, finish):
                for g in range(4):
                    for c in range(3):
                        exp_chunk(i, g, c)
                        if isinstance(i, int) and i == 0 and (g, c) == (0, 0):
                            mid_part(B - 1, (B - 1) % 2)
                        if finish and (g, c) == (1, 0):
                            take_o(i - 1, 1)
                        if (g, c) == (3, 0):
                            take_o(i, 0)
                        if finish and (g, c) == (3, 1):
                            take_ont(i - 1)

            step(0, False)
            with act.Fori(0, 3) as t:
                step(2 * t + 1, True)
                step(2 * t + 2, True)
            for n in range(CH):
                exp_chunk(7, n // 3, n % 3)
                if n == 2:
                    take_o(6, 1)
                if n == 6:
                    take_ont(6)
                if n == 9:
                    take_o(7, 0)
            act.wait_ge(pb_done, 1)
            nc.scalar.activation(warm[:, :], pbias[:, :], ACT.Gelu_apprx_tanh)
            take_o(7, 1)

            def late_q(u):
                j, c0, c1 = UNITS[u]
                act.wait_ge(q_done, u + 1)
                act.wait_ge(y_done, u - 1)
                nc.scalar.activation(Q4[u % 2][:, 0:c1 - c0], O_ps[u % 2][:, 0:c1 - c0], ACT.Copy)\
                    .then_inc(q_taken[u % 2], 1)

            for u, (j, c0, c1) in enumerate(UNITS):
                for f in range(NF):
                    n = NF * u + f
                    act.wait_ge(h_done, n + 1)
                    if u >= 2:
                        act.wait_ge(q_done, u - 1)
                    nc.scalar.activation(H[u % 2][f][:, 0:c1 - c0], last_ps[n % 3][:, 0:c1 - c0], ACT.Gelu_apprx_tanh,
                                         bias=F("b1")[:, f:f + 1]).then_inc(gelu_done, 1)
                    if (u, f) == (1, 0):
                        take_ont(7)
                    if (u, f) == (4, 1):
                        late_q(3)
            late_q(4)

        @block.vector
        def _(dve):
            dve.wait_ge(cond_in, 16)
            nc.vector.max(top[:, :], cond_sb[:, :]).then_inc(top_done, 1)
            dve.wait_ge(top_done, 1)
            nc.vector.max_index(expert[:, :], top[:, :], cond_sb[:, :]).then_inc(expert_done, 1)

            def silu(b, p):
                dve.wait_ge(sig_done, 2 * b + 2)
                for h in range(HC):
                    cols = slice(h * SEQ, (h + 1) * SEQ)
                    nc.vector.scalar_tensor_tensor(out=silu_up[p][:, cols], in0=up_ps[p][:, cols],
                                                   scalar=wexp[b][:, BU0 + h:BU0 + h + 1], in1=sig_up[p][:, cols],
                                                   op0=ALU.add, op1=ALU.mult).then_inc(silu_done, 1)

            def hide(b, p):
                dve.wait_ge(silu_done, 2 * b + 2)
                dve.wait_ge(gate_done, b + 1)
                for h in range(HC):
                    cols = slice(h * SEQ, (h + 1) * SEQ)
                    last = nc.vector.scalar_tensor_tensor(out=hidden[p][:, cols], in0=gate_ps[:, cols],
                                                          scalar=wexp[b][:, BG0 + h:BG0 + h + 1],
                                                          in1=silu_up[p][:, cols], op0=ALU.add, op1=ALU.mult)
                last.then_inc(hid_done, 1)

            def take_v(b, p):
                dve.wait_ge(vmm_done, b + 1)
                wait(dve, staged[b % STAGES], 2 * 16 * (b // STAGES))
                nc.vector.tensor_tensor(vrow[b % STAGES][:, :].rearrange("p (t n) -> p t n", t=NT),
                                        v_ps[:, 0:NT * D].rearrange("p (t n) -> p t n", t=NT),
                                        A("bv").rearrange("p (a n) -> p a n", a=1).broadcast_to([128, NT, D]),
                                        ALU.add).then_inc(v_taken, 1)

            def stack_v1():
                dve.wait_ge(v1_done, 4)
                dve.wait_ge(zero_done, 3)
                nc.vector.tensor_copy(v1_first[0:96, :], v1_parts[0:96, 0, :])
                nc.vector.tensor_copy(v1_first[96:128, :], v1_parts[96:128, 1, :])
                nc.vector.tensor_copy(v1_second[0:32, :], v1_parts[0:32, 2, :])
                nc.vector.tensor_copy(v1_second[32:64, :], v1_parts[32:64, 1, :]).then_inc(v1_stacked, 1)

            def weigh_lora():
                dve.wait_ge(lm_taken, 1)
                nc.vector.tensor_tensor(lora_w[:, :].rearrange("p (b r) -> p b r", b=B),
                                        lora_m[:, :].rearrange("p (a r) -> p a r", a=1).broadcast_to([128, B, RANK]),
                                        F("cond").rearrange("p (b a) -> p b a", a=1).broadcast_to([128, B, RANK]),
                                        ALU.mult).then_inc(lw_done, 1)

            def reduce_chunk(i, p, g, c):
                n = 3 * g + c
                part, full, pair, _ = chunk_kind("S", g // 2, c)
                wait(dve, s_done, CH * i + n + 1)
                cols = mx[p][:, :].rearrange("p (h t) -> p h t", t=NT)
                if full:
                    head = 4 * g + 2 * pair
                    out = cols[:, head:head + 2, part]
                    src = S_ps[n % 2][:, :].rearrange("p (h s) -> p h s", h=2)
                else:
                    out = cols[:, 4 * g:4 * g + 4, part]
                    src = S_ps[n % 2][:, :].rearrange("p (h s) -> p h s", h=4)
                if n in (0, 6):
                    wait(dve, mt_done[n // 6], i - 1)
                nc.vector.tensor_reduce(out, src, AX.X, ALU.max).then_inc(max_done, 1)

            def split_max(i, h):
                wait(dve, mt_done[h], i + 1)
                wait(dve, mrow_in[h], 32 * i)
                nc.vector.tensor_scalar(mrow[h][:, 0, :], turned_max, -1.0, None, ALU.mult)\
                    .then_inc(mt_hi[h], 1)
                wait(dve, mt_hi[h], i + 1)
                nc.vector.scalar_tensor_tensor(out=mrow[h][:, 1, :], in0=turned_max, scalar=-1.0,
                                               in1=mrow[h][:, 0, :], op0=ALU.mult, op1=ALU.subtract)\
                    .then_inc(mt_taken[h], 1)

            def normalise(i, h):
                wait(dve, dt_done[h], i + 1)
                src = M_ps[h][:, 0:SEQ].rearrange("p (n u) -> p n u", u=32)
                rd = rden[h][:, :].rearrange("p (n a) -> p n a", a=2)
                nc.vector.reciprocal(rd, src[:, :, 16:32:HD]).then_inc(rden_done[h], 1)
                wait(dve, rden_done[h], i + 1)
                nc.vector.tensor_tensor(
                    On[:, :, h * 64:(h + 1) * 64].rearrange("p t (j a d) -> p t j a d", a=2, d=HD),
                    M_ps[h][:, 0:SEQ].rearrange("p (t j b a d) -> p t j b a d", t=NT, b=2, a=2, d=HD)[:, :, :, 0, :, :],
                    rden[h][:, :].rearrange("p (t j a o) -> p t j a o", t=NT, a=2, o=1)
                    .broadcast_to([128, NT, 4, 2, HD]),
                    ALU.mult).then_inc(dt_taken[h], 1)

            def residual(i):
                wait(dve, wf_done, i + 1)
                nc.vector.scalar_tensor_tensor(out=x1[:, bass.ds(i * SEQ, SEQ)], in0=M_ps[0][:, 0:SEQ],
                                               scalar=A("bf"), in1=xT[:, bass.ds(i * SEQ, SEQ)],
                                               op0=ALU.add, op1=ALU.add).then_inc(x1_done, 1)

            def step(i, p, ahead, now, finish):
                for g in range(4):
                    for c in range(3):
                        if ahead:
                            reduce_chunk(i + 1, 1 - p, g, c)
                        if now and (g, c) == (0, 0):
                            split_max(i, 1)
                        if ahead and (g, c) == (2, 1):
                            split_max(i + 1, 0)
                    if finish and g == 1:
                        normalise(i - 1, 0)
                        normalise(i - 1, 1)
                if finish:
                    residual(i - 1)

            def reduce_first_batch(k, c):
                n = 3 * k + c - S0_PLACE
                if 0 <= n < CH:
                    reduce_chunk(0, 0, n // 3, n % 3)

            for k in range(B + 1):
                reduce_first_batch(k, 0)
                if k < B:
                    silu(k, k % 2)
                if k == MAX_AT:
                    split_max(0, 0)
                if k < B:
                    hide(k, k % 2)
                if k == 2:
                    weigh_lora()
                if k == 0:
                    dve.wait_ge(pa_in, 16)
                    nc.vector.tensor_scalar(bq_scaled[:, :], A("bq"), SCALE, None, ALU.mult).then_inc(bq_done, 1)
                reduce_first_batch(k, 1)
                if 1 <= k <= B:
                    take_v(k - 1, (k - 1) % 2)
                reduce_first_batch(k, 2)
            step(0, 0, True, True, False)
            with dve.Fori(0, 3) as t:
                step(2 * t + 1, 1, True, True, True)
                step(2 * t + 2, 0, True, True, True)

            def split_p(rows, cols, n, products):
                dve.wait_ge(p_done, products)
                nc.vector.tensor_scalar(Pparts[rows, 0, cols], S_ps[0][rows, cols], pbias[rows, 0:1], None, ALU.add)\
                    .then_inc(p_split, 1)
                dve.wait_ge(p_split, 4 * n + 1)
                nc.vector.scalar_tensor_tensor(out=Prest[rows, cols], in0=S_ps[0][rows, cols],
                                               scalar=pbias[rows, 0:1], in1=Pparts[rows, 0, cols],
                                               op0=ALU.add, op1=ALU.subtract).then_inc(p_split, 1)
                dve.wait_ge(p_split, 4 * n + 2)
                nc.vector.tensor_copy(Pparts[rows, 1, cols], Prest[rows, cols]).then_inc(p_split, 1)
                dve.wait_ge(p_split, 4 * n + 3)
                nc.vector.tensor_tensor(Pparts[rows, 2, cols], Prest[rows, cols], Pparts[rows, 1, cols], ALU.subtract)\
                    .then_inc(p_split, 1)

            def stack_p(u, splits):
                j, c0, c1 = UNITS[u]
                dve.wait_ge(p_split, 4 * splits)
                for s, part in enumerate((0, 1, 2, 0)):
                    last = nc.vector.tensor_copy(Pstack[j][32 * s:32 * s + 32, c0:c1],
                                                 Pparts[32 * j:32 * j + 32, part, c0:c1])
                last.then_inc(stack_done, 1)

            def take_q(u):
                j, c0, c1 = UNITS[u]
                dve.wait_ge(q_done, u + 1)
                if u >= 2:
                    dve.wait_ge(y_done, u - 1)
                nc.vector.tensor_copy(Q4[u % 2][:, 0:c1 - c0], O_ps[u % 2][:, 0:c1 - c0])\
                    .then_inc(q_taken[u % 2], 1)

            def finish(u):
                j, c0, c1 = UNITS[u]
                dve.wait_ge(y_done, u + 1)
                if u >= 2:
                    dve.wait_ge(out_done[u % 2], 16 * (u // 2))
                nc.vector.scalar_tensor_tensor(
                    out=Y[u % 2][:, 0:c1 - c0].rearrange("p (q s) -> p q s", s=SEQ),
                    in0=M_ps[1 - u % 2][:, 0:c1 - c0].rearrange("p (q s) -> p q s", s=SEQ), scalar=F("b2"),
                    in1=x1[:, :].rearrange("p (q j s) -> p q j s", q=2, j=4)[:, c0 // SEQ:c1 // SEQ, j, :],
                    op0=ALU.add, op1=ALU.add).then_inc(y_taken, 1)

            split_max(7, 1)
            split_p(slice(0, 128), slice(0, SEQ), 0, 1)
            normalise(6, 0)
            normalise(6, 1)
            split_p(slice(0, 64), slice(SEQ, 2 * SEQ), 1, 1)
            stack_p(0, 2)
            stack_v1()
            residual(6)
            stack_p(1, 2)
            split_p(slice(64, 96), slice(SEQ, 2 * SEQ), 2, 2)
            normalise(7, 0)
            normalise(7, 1)
            stack_p(2, 2)
            stack_p(3, 3)
            residual(7)
            take_q(0)
            split_p(slice(96, 128), slice(SEQ, 2 * SEQ), 3, 3)
            stack_p(4, 4)
            take_q(1)
            finish(0)
            take_q(2)
            for u in range(1, 5):
                finish(u)

        @block.tensor
        def _(pe):
            def up(b, p):
                pe.wait_ge(w_in[b], 16)
                if b in (0, 4):
                    pe.wait_ge(x_in[b // 4], 16)
                wait(pe, silu_done, 2 * (b - 1))
                for h in range(HC):
                    last = nc.tensor.matmul(up_ps[p][:, h * SEQ:(h + 1) * SEQ],
                                            wexp[b][:, WU0 + h * 128:WU0 + (h + 1) * 128],
                                            xT[:, b * SEQ:(b + 1) * SEQ], start=True, stop=True)
                last.then_inc(up_done, 1)

            def gate(b, p):
                if b == 0:
                    pe.wait_ge(w_rest_in, 16)
                wait(pe, hid_done, b)
                for h in range(HC):
                    last = nc.tensor.matmul(gate_ps[:, h * SEQ:(h + 1) * SEQ],
                                            wexp[b][:, WG0 + h * 128:WG0 + (h + 1) * 128],
                                            xT[:, b * SEQ:(b + 1) * SEQ], start=True, stop=True)
                last.then_inc(gate_done, 1)

            def down(b, p):
                pe.wait_ge(hid_done, b + 1)
                wait(pe, c_taken, b)
                for h in range(HC):
                    last = nc.tensor.matmul(c_ps[:, 0:SEQ], wexp[b][:, WD0 + h * 128:WD0 + (h + 1) * 128],
                                            hidden[p][:, h * SEQ:(h + 1) * SEQ], start=(h == 0), stop=(h == HC - 1))
                last.then_inc(down_done, 1)

            def project(b, p):
                if b == 0:
                    pe.wait_ge(pa_in, 16)
                pe.wait_ge(c_taken, b + 1)
                wait(pe, qk32_done, 2 * b)
                nc.tensor.matmul(qk_ps[:, 0:SEQ], A("wq"), cT[p][:, :], start=True, stop=True)
                nc.tensor.matmul(qk_ps[:, SEQ:2 * SEQ], A("wk"), cT[p][:, :], start=True, stop=True)\
                    .then_inc(qkmm_done, 1)
                wait(pe, v_taken, b)
                if b == MAX_AT - 1:
                    pe.wait_ge(mt_taken[0], 1)
                for t in range(NT):
                    last = nc.tensor.matmul(v_ps[:, t * D:(t + 1) * D], cT[p][:, t * 128:(t + 1) * 128], A("wv"),
                                            start=True, stop=True)
                last.then_inc(vmm_done, 1)

            def fold_lora():
                pe.wait_ge(pf_in, 16)
                nc.tensor.matmul(S_ps[0][:, 0:RANK], F("lora_b"), F("u1")[:, 0:RANK], start=True, stop=True)\
                    .then_inc(lm_done, 1)

            def fold_base():
                pe.wait_ge(lw_done, 1)
                nc.tensor.matmul(S_ps[1][:, 0:B * RANK], F("lora_a"), lora_w[:, :], start=True, stop=False)
                nc.tensor.matmul(S_ps[1][:, 0:B * RANK], F("base"), F("u1"), start=False, stop=True).then_inc(g_done, 1)
                pe.wait_ge(lm_taken, 1)
                nc.tensor.matmul(S_ps[0][:, 64:65], F("u1")[:, 0:128], F("b_base"), start=True, stop=True)\
                    .then_inc(g_done, 1)

            def scores(side, ps, stationary, moving, rows, g, c):
                part, full, pair, mask = chunk_kind(side, g // 2, c)
                nh = 2 if full else 4
                view = ps[:, :].rearrange("p (h s) -> p h s", h=nh)
                diag = view[:, :, part * 128:(part + 1) * 128] if full else view
                nc.tensor.matmul(diag, ident_b, mask.rearrange("p (a s) -> p a s", a=1).broadcast_to([128, nh, 128]),
                                 start=True, stop=False, skip_group_check=True)
                for n in range(nh):
                    head = 4 * g + (2 * pair if full else 0) + n
                    rhs = moving[0:rows, head, :] if full else moving[0:rows, head, part * 128:(part + 1) * 128]
                    last = nc.tensor.matmul(view[:, n, :], stationary[0:rows, head, part * 128:(part + 1) * 128], rhs,
                                            start=False, stop=(n == nh - 1), skip_group_check=True)
                return last

            def s_chunk(i, p, g, c, count):
                n = 3 * g + c
                if n in (0, 6):
                    pe.wait_ge(qk_in[n // 6][p], (1 + PARTS) * 16 * count)
                wait(pe, max_done, CH * i + n - 1)
                scores("S", S_ps[n % 2], QS[p], KS[p], R_MAXROW, g, c).then_inc(s_done, 1)

            def s_first_batch(k, c):
                n = 3 * k + c - S0_PLACE
                if 0 <= n < CH:
                    s_chunk(0, 0, n // 3, n % 3, 1)

            def s_first():
                pe.wait_ge(g_taken, 1)
                pe.wait_ge(pb_done, 1)
                pe.wait_ge(cb_in, 16)
                pe.wait_ge(const_in, 64)

            def t_chunk(i, p, g, c):
                n = 3 * g + c
                if n in (0, 6):
                    wait(pe, mrow_in[n // 6], 32 * (i + 1))
                if isinstance(i, int) and i == B - 1 and n >= 2:
                    wait(pe, exp_done, CH * i + n - 2 if n > 2 else 0)
                    scores("T", last_ps[n % 3], KS[p], QS[p], R_ALL, g, c).then_inc(t_done, 1)
                    return
                wait(pe, exp_done, CH * i + n - 1)
                scores("T", T_ps[n % 2], KS[p], QS[p], R_ALL, g, c).then_inc(t_done, 1)

            def pv(i, p, g):
                h = g // 2
                if g == 0:
                    wait(pe, va_done, 2 * i + 2)
                if g % 2 == 0:
                    wait(pe, o_taken[h], i)
                wait(pe, exp_done, CH * i + 3 * g + 3)
                for c, part in ((0, h), (2, 1 - h)):
                    for j in range(4):
                        v = vaug[p][:, part, 4 * g + j, :]
                        if c == 0:
                            last = nc.tensor.matmul(O_ps[h][32 * j:32 * j + 32, 0:SEQ], v,
                                                    PB[g][j // 2][:, (j % 2) * SEQ:(j % 2 + 1) * SEQ],
                                                    start=(g % 2 == 0), stop=False, skip_group_check=True)
                        else:
                            last = nc.tensor.matmul(O_ps[h][32 * j:32 * j + 32, part * 128:(part + 1) * 128], v,
                                                    PB[g][2][:, j * 128:(j + 1) * 128],
                                                    start=False, stop=(g % 2 == 1), skip_group_check=True)
                last.then_inc(pv_done, 1)

            def turn_max(i, p, h):
                wait(pe, max_done, CH * i + 6 * (h + 1))
                if h == 1:
                    wait(pe, mt_taken[0], i + 1)
                    if isinstance(i, int) and i == 0:
                        pe.wait_ge(v_taken, B)
                else:
                    wait(pe, dt_taken[1], i - 1)
                nc.tensor.transpose(turned_max, mx[p][:, h * HALF * NT:(h + 1) * HALF * NT], A("ident"))\
                    .then_inc(mt_done[h], 1)

            def turn_o(i, h):
                wait(pe, o_taken[h], i + 1)
                if h == 1:
                    wait(pe, mt_taken[1], min(i + 2, B) if isinstance(i, int) else i + 2)
                for t in range(NT):
                    last = nc.tensor.transpose(M_ps[h][:, t * 128:(t + 1) * 128], OS[h][:, t * 128:(t + 1) * 128],
                                               A("ident"))
                last.then_inc(dt_done[h], 1)

            def turn_on(i):
                for h in range(2):
                    wait(pe, dt_taken[h], i + 1)
                for t in range(NT):
                    last = nc.tensor.transpose(M_ps[0][:, t * 128:(t + 1) * 128], On[:, t, :], A("ident"))
                last.then_inc(ont_done, 1)

            def out_project(i):
                wait(pe, ont_taken, i + 1)
                nc.tensor.matmul(M_ps[0][:, 0:SEQ], A("wf"), OnT[:, :], start=True, stop=True).then_inc(wf_done, 1)

            def step(i, p, count, ahead, now, finish):
                for g in range(4):
                    for c in range(3):
                        if ahead:
                            s_chunk(i + 1, 1 - p, g, c, count)
                        if now:
                            t_chunk(i, p, g, c)
                        if now and (g, c) == (0, 0):
                            turn_max(i, p, 1)
                        if ahead and (g, c) == (2, 1):
                            turn_max(i + 1, 1 - p, 0)
                    if finish and g == 0:
                        pv(i - 1, 1 - p, 3)
                    if finish and g == 1:
                        turn_o(i - 1, 0)
                        turn_o(i - 1, 1)
                    if finish and g == 2:
                        turn_on(i - 1)
                    if now and g >= 1:
                        pv(i, p, g - 1)
                if finish:
                    out_project(i - 1)

            def warm_up(times):
                for _ in range(times):
                    nc.tensor.matmul(S_ps[0][:, :], v1_second[:, 0:128], v1_second[:, :], start=True, stop=True)

            pe.wait_ge(zero_done, 1)
            warm_up(12)
            for k in range(B + 1):
                if k < B:
                    up(k, k % 2)
                if k == 2:
                    fold_lora()
                if k == 3:
                    fold_base()
                if k == S0_PLACE // 3:
                    s_first()
                s_first_batch(k, 0)
                if k >= 1:
                    down(k - 1, (k - 1) % 2)
                if k == MAX_AT:
                    pe.wait_ge(v_taken, k - 1)
                    turn_max(0, 0, 0)
                if k < B:
                    gate(k, k % 2)
                s_first_batch(k, 1)
                if k >= 1:
                    project(k - 1, (k - 1) % 2)
                s_first_batch(k, 2)
            step(0, 0, 1, True, True, False)
            pe.wait_ge(qk32_done, 2 * B)
            with pe.Fori(0, 3) as t:
                step(2 * t + 1, 1, t + 2, True, True, True)
                step(2 * t + 2, 0, t + 2, True, True, True)

            def low_rank(b):
                j, q = b % 4, b // 4
                return nc.tensor.matmul(S_ps[0][32 * j:32 * j + 32, q * SEQ:(q + 1) * SEQ],
                                        G[:, b * RANK:(b + 1) * RANK], x1[:, b * SEQ:(b + 1) * SEQ],
                                        start=(q == 0), stop=True, skip_group_check=True)

            def ff_up(u, f0, f1):
                j, c0, c1 = UNITS[u]
                pe.wait_ge(stack_done, u + 1)
                for f in range(f0, f1):
                    n = NF * u + f
                    if n < 3:
                        pe.wait_ge(exp_done, CH * B - 2 + n)
                    else:
                        pe.wait_ge(gelu_done, n - 2)
                    for w in (v1_first, v1_second):
                        last = nc.tensor.matmul(last_ps[n % 3][:, 0:c1 - c0], w[:, f * 128:(f + 1) * 128],
                                                Pstack[j][:, c0:c1], start=(w is v1_first), stop=(w is v1_second))
                    last.then_inc(h_done, 1)

            def ff_rank(u):
                j, c0, c1 = UNITS[u]
                pe.wait_ge(gelu_done, NF * (u + 1))
                if u < 2:
                    pe.wait_ge(o_taken[u], B)
                else:
                    pe.wait_ge(q_taken[u % 2], u // 2)
                for f in range(NF):
                    last = nc.tensor.matmul(O_ps[u % 2][32 * f:32 * f + 32, 0:c1 - c0], u2[:, f, :],
                                            H[u % 2][f][:, 0:c1 - c0], start=True, stop=True)
                last.then_inc(q_done, 1)

            def ff_down(u):
                j, c0, c1 = UNITS[u]
                pe.wait_ge(q_taken[u % 2], u // 2 + 1)
                if u >= 2:
                    pe.wait_ge(y_taken, u - 1)
                nc.tensor.matmul(M_ps[1 - u % 2][:, 0:c1 - c0], F("v2"), Q4[u % 2][:, 0:c1 - c0],
                                 start=True, stop=True).then_inc(y_done, 1)

            def last_t(n):
                t_chunk(7, 1, n // 3, n % 3)

            last_t(0)
            last_t(1)
            turn_max(7, 1, 1)
            pv(6, 0, 3)
            pe.wait_ge(max_done, CH * B)
            last_t(2)
            pe.wait_ge(x1_done, 6)
            for b in range(6):
                last = low_rank(b)
            last.then_inc(p_done, 1)
            last_t(3)
            last_t(4)
            turn_o(6, 0)
            turn_o(6, 1)
            last_t(5)
            pv(7, 1, 0)
            last_t(6)
            last_t(7)
            turn_on(6)
            last_t(8)
            pv(7, 1, 1)
            out_project(6)
            last_t(9)
            last_t(10)
            pv(7, 1, 2)
            last_t(11)
            pe.wait_ge(x1_done, 7)
            pe.wait_ge(p_split, 6)
            low_rank(6).then_inc(p_done, 1)
            pe.wait_ge(v1_stacked, 1)
            ff_up(0, 0, 1)
            pv(7, 1, 3)
            ff_up(0, 1, 3)
            turn_o(7, 0)
            turn_o(7, 1)
            ff_up(0, 3, NF)
            ff_up(1, 0, 1)
            turn_on(7)
            ff_up(1, 1, NF)
            out_project(7)
            ff_rank(0)
            pe.wait_ge(x1_done, B)
            pe.wait_ge(p_split, 10)
            low_rank(7).then_inc(p_done, 1)
            ff_up(2, 0, NF)
            ff_rank(1)
            ff_up(3, 0, 2)
            ff_down(0)
            ff_up(3, 2, NF)
            ff_rank(2)
            ff_down(1)
            ff_up(4, 0, 2)
            ff_rank(3)
            ff_up(4, 2, NF)
            ff_down(2)
            ff_down(3)
            ff_rank(4)
            ff_down(4)


def _packed(inputs):
    import numpy as np

    f32 = np.float32
    g = {k: np.asarray(v) for k, v in inputs.items()}
    xT = np.ascontiguousarray(g["x"].reshape(B * SEQ, D).T)

    def hidden_bias(v):
        return v.reshape(EXPERTS, HC, 128).transpose(0, 2, 1)

    wexp = np.concatenate([
        hidden_bias(g["L0_cond_b_up"]), hidden_bias(g["L0_cond_b_gate"]), g["L0_cond_b_down"][:, :, None],
        g["L0_cond_W_up"].transpose(0, 2, 1), g["L0_cond_W_gate"].transpose(0, 2, 1),
        g["L0_cond_W_down"].reshape(EXPERTS, D, HC, 128).transpose(0, 3, 2, 1).reshape(EXPERTS, 128, HC * D)], axis=2)

    def by_d(w):
        return w.reshape(w.shape[:-1] + (HEADS, HD)).swapaxes(-1, -2).reshape(w.shape)

    wf = g["L0_attn_Wf"].reshape(2, 2, 4, HD, D).swapaxes(1, 2).reshape(D, D)

    pa = np.concatenate([
        by_d(g["L0_attn_Wq"]), by_d(g["L0_attn_Wk"]), g["L0_attn_Wv"], wf, np.eye(128, dtype=f32),
        np.tile(g["L0_attn_bv"][None], (128, 1)), by_d(g["L0_attn_bq"])[:, None], by_d(g["L0_attn_bk"])[:, None],
        g["L0_attn_bf"][:, None]], axis=1)

    pf = np.concatenate([
        g["L0_cond2_W_base"], g["L0_cond2_Bs"].transpose(1, 0, 2).reshape(D, EXPERTS * RANK_L),
        g["L0_cond2_As"].reshape(EXPERTS * RANK_L, D), np.tile(g["L0_ffn_U1"], (1, B)),
        g["L0_cond2_b_base"][:, None], np.repeat(g["cond_8"].T, RANK_L, axis=0), g["L0_ffn_b1"].reshape(NF, 128).T,
        g["L0_ffn_U2"].reshape(NF, 128, RANK).transpose(1, 0, 2).reshape(128, NF * RANK),
        np.tile(g["L0_ffn_V2"], (NF, 1)), g["L0_ffn_b2"][:, None], np.tile(g["L0_ffn_V1"], (4, 1))], axis=1)

    bf = np.dtype("bfloat16")
    neg = f32(-1e9)
    tri = np.arange(128)
    cb = np.concatenate([np.eye(128, dtype=f32), np.where(tri[None] > tri[:, None], neg, f32(0)),
                         np.where(tri[None] < tri[:, None], neg, f32(0))], axis=1).astype(bf)

    base = 24.0 ** (1.0 / HALF)
    slope = (f32(1.0) / f32(base) ** np.arange(1, HALF + 1, dtype=f32)).astype(f32)
    signed = np.concatenate([slope, -slope])
    three = []
    left = signed.copy()
    for _ in range(3):
        three.append(left.astype(bf).astype(f32))
        left = left - three[-1]
    pos = np.arange(SEQ, dtype=f32)
    qc = np.zeros((R_CONST, HEADS, SEQ), f32)
    kc = np.zeros((R_CONST, HEADS, SEQ), f32)
    for n, s in enumerate(three):
        qc[n], kc[n] = s[:, None], pos[None]
        qc[3 + n], kc[3 + n] = -pos[None], s[:, None]
    kc[R_MAXROW - R_STACK:] = 1.0
    return [xT, wexp, g["cond_8"], pa, pf, cb, qc.astype(bf), kc.astype(bf)]


_INS = ["xT", "wexp", "cond", "pa", "pf", "cb", "qc", "kc"]


def kernel(**inputs):
    import numpy as _np
    import concourse.bacc as _bacc
    from concourse import mybir as _mybir
    from concourse.bass_utils import run_bass_kernel_spmd as _run

    nc = _bacc.Bacc("TRN2", target_bir_lowering=False, num_devices=1)
    arrays, args = {}, []
    for name, a in zip(_INS, _packed(inputs)):
        a = _np.ascontiguousarray(a)
        arrays[f"in_{name}_dram"] = a
        args.append(nc.dram_tensor(f"in_{name}_dram", a.shape, _mybir.dt.from_np(a.dtype), kind="ExternalInput").ap())
    args.append(nc.dram_tensor("out_0_dram", (D, B * SEQ), _mybir.dt.float32, kind="ExternalOutput").ap())
    adaln_attention_ffn(nc, *args)
    r = _run(nc, [arrays], core_ids=[0])
    got = r.results[0]["out_0_dram"]
    return _np.ascontiguousarray(_np.asarray(got).T).reshape(B, SEQ, D)
```
